# Optimizing a Trainium2 kernel written in Bass

```python
import numpy as np
import jax
import jax.numpy as jnp

def _softmax(x, axis=-1):
    return jax.nn.softmax(x, axis=axis)

def _gelu(x):
    return jax.nn.gelu(x, approximate=True)

def _silu(x):
    return jax.nn.silu(x)

def _sigmoid(x):
    return jax.nn.sigmoid(x)

def _layernorm(x, axis=-1, eps=1e-05):
    m = jnp.mean(x, axis=axis, keepdims=True)
    v = jnp.var(x, axis=axis, keepdims=True)
    return (x - m) / jnp.sqrt(v + eps)

def _scatter_add(tgt, idx, src, axis=0):
    return tgt.at[idx].add(src)

def _segment_sum(src, seg, n):
    return jax.ops.segment_sum(src, seg, n)
kernel_name = 'mk_cond_resid_d4_seqx_r2_0e01d8'

def setup_inputs(seed: int=0):
    np.random.seed(seed)
    _w = jnp.asarray

    def _rec_inputs():
        import jax
        import jax.numpy as jnp
        _rk = jax.random.key(seed)
        x = -0.0003929 + 0.9999 * jax.random.normal(jax.random.fold_in(_rk, 1), (128, 128, 512), jnp.float32)
        _lenS = 128 - jax.random.randint(jax.random.fold_in(_rk, 7), (128,), 0, max(1, 128 // 4) + 1, jnp.int32)
        _lenS2 = 128 - jax.random.randint(jax.random.fold_in(_rk, 8), (128,), 0, max(1, 128 // 4) + 1, jnp.int32)
        itok_B_0_7 = jax.random.randint(jax.random.fold_in(_rk, 11), (128,), 0, 8, jnp.int32)
        condB_deltat = jax.random.uniform(jax.random.fold_in(_rk, 12), (128,), jnp.float32, 0.0, 1.99976)
        itok_B_0_63 = jax.random.randint(jax.random.fold_in(_rk, 13), (128,), 0, 64, jnp.int32)
        itok_B_0_8 = jax.random.randint(jax.random.fold_in(_rk, 14), (128,), 0, 9, jnp.int32)
        return (x, itok_B_0_7, condB_deltat, itok_B_0_63, itok_B_0_8)
    x, itok_B_0_7, condB_deltat, itok_B_0_63, itok_B_0_8 = _rec_inputs()

    def _L0_cond_setup():
        import jax, jax.numpy as jnp
        import numpy as np
        S, O, H = (8, 512, 512)
        B, N = (32, 256)
        key = jax.random.key(seed)
        k1, k2, k3, k4 = jax.random.split(key, 4)
        x = jax.random.normal(k1, (B, N, H), dtype=jnp.float32)
        subject_id = jax.random.randint(k2, (B,), 0, S)
        wbound = jnp.sqrt(2.0 / 6.0) * jnp.sqrt(3.0 / H)
        weight = jax.random.uniform(k3, (S, O, H), minval=-wbound, maxval=wbound, dtype=jnp.float32)
        bbound = 1.0 / jnp.sqrt(H)
        bias = jax.random.uniform(k4, (S, O), minval=-bbound, maxval=bbound, dtype=jnp.float32)
        return {'x': x, 'subject_id': subject_id, 'weight': weight, 'bias': bias}
    _L0_cond_all = _L0_cond_setup()
    _L0_cond_in = {k: v for k, v in _L0_cond_all.items() if k in ('weight', 'bias')}
    del _L0_cond_all

    def _L1_cond_setup():
        import jax, jax.numpy as jnp
        import numpy as np
        B, F, T = (128, 64, 512)
        key = jax.random.key(seed)
        k1, k2, k3, k4 = jax.random.split(key, 4)
        x = jax.random.normal(k1, (B, 2 * F, T), dtype=jnp.float32)
        delta_t = jax.random.uniform(k2, (B,), dtype=jnp.float32, minval=0.5, maxval=2.0)
        amplitudes = jax.random.uniform(k3, (F,), dtype=jnp.float32, minval=0.7, maxval=1.3)
        frequencies = jax.random.uniform(k4, (F,), dtype=jnp.float32, minval=0.0, maxval=2.0 * np.pi)
        return {'x': x, 'delta_t': delta_t, 'amplitudes': amplitudes, 'frequencies': frequencies}
    _L1_cond_all = _L1_cond_setup()
    _L1_cond_in = {k: v for k, v in _L1_cond_all.items() if k in ('amplitudes', 'frequencies')}
    del _L1_cond_all

    def _L2_cond_setup():
        import jax, jax.numpy as jnp
        import numpy as np
        NUM_CATEGORIES = 64
        INPUT_DIM = 512
        HIDDEN_DIM = 512
        B = 128
        S = 64
        key = jax.random.key(seed)
        kx, kc, kw = jax.random.split(key, 3)
        x = jax.random.normal(kx, (B, S, INPUT_DIM), dtype=jnp.float32)
        cat_ids = jax.random.randint(kc, (B,), 0, NUM_CATEGORIES, dtype=jnp.int32)
        W = 0.02 * jax.random.normal(kw, (NUM_CATEGORIES, INPUT_DIM, HIDDEN_DIM), dtype=jnp.float32)
        b = jnp.zeros((NUM_CATEGORIES, HIDDEN_DIM), dtype=jnp.float32)
        return {'x': x, 'cat_ids': cat_ids, 'W': W, 'b': b}
    _L2_cond_all = _L2_cond_setup()
    _L2_cond_in = {k: v for k, v in _L2_cond_all.items() if k in ('W', 'b')}
    del _L2_cond_all

    def _L3_cond_setup():
        import jax, jax.numpy as jnp
        import numpy as np
        LN_EPS = 1e-05
        key = jax.random.key(seed)
        ks = jax.random.split(key, 8)
        B, S, H, A, L = (32, 1024, 512, 128, 10)
        return {'hidden_states': jax.random.normal(ks[0], (B, S, H), dtype=jnp.float32), 'language_ids': jax.random.randint(ks[1], (B,), 0, L, dtype=jnp.int64), 'W1': jax.random.normal(ks[2], (L, H, A), dtype=jnp.float32) * (1.0 / np.sqrt(H)), 'b1': jnp.zeros((L, A), dtype=jnp.float32), 'W2': jax.random.normal(ks[3], (L, A, H), dtype=jnp.float32) * (1.0 / np.sqrt(A)), 'b2': jnp.zeros((L, H), dtype=jnp.float32), 'gamma': jnp.ones((L, H), dtype=jnp.float32), 'beta': jnp.zeros((L, H), dtype=jnp.float32)}
    _L3_cond_all = _L3_cond_setup()
    _L3_cond_in = {k: v for k, v in _L3_cond_all.items() if k in ('W1', 'b1', 'W2', 'b2', 'gamma', 'beta')}
    del _L3_cond_all
    return {'x': x, 'itok_B_0_7': itok_B_0_7, 'condB_deltat': condB_deltat, 'itok_B_0_63': itok_B_0_63, 'itok_B_0_8': itok_B_0_8, 'L0_cond_weight': _L0_cond_in['weight'], 'L0_cond_bias': _L0_cond_in['bias'], 'L1_cond_amplitudes': _L1_cond_in['amplitudes'], 'L1_cond_frequencies': _L1_cond_in['frequencies'], 'L2_cond_W': _L2_cond_in['W'], 'L2_cond_b': _L2_cond_in['b'], 'L3_cond_W1': _L3_cond_in['W1'], 'L3_cond_b1': _L3_cond_in['b1'], 'L3_cond_W2': _L3_cond_in['W2'], 'L3_cond_b2': _L3_cond_in['b2'], 'L3_cond_gamma': _L3_cond_in['gamma'], 'L3_cond_beta': _L3_cond_in['beta']}

def reference(x, itok_B_0_7, condB_deltat, itok_B_0_63, itok_B_0_8, L0_cond_weight, L0_cond_bias, L1_cond_amplitudes, L1_cond_frequencies, L2_cond_W, L2_cond_b, L3_cond_W1, L3_cond_b1, L3_cond_W2, L3_cond_b2, L3_cond_gamma, L3_cond_beta):
    import jax
    import jax.numpy as jnp

    def _L0_cond_ref(x, subject_id, weight, bias):
        import jax, jax.numpy as jnp
        import numpy as np
        S, O, H = (8, 512, 512)
        B, N = (32, 256)
        W = weight[subject_id]
        b = bias[subject_id]
        y = jnp.einsum('bnh,boh->bno', x, W) + b[:, None, :]
        return y

    def _L1_cond_ref(x, delta_t, amplitudes, frequencies):
        import jax, jax.numpy as jnp
        import numpy as np
        B, F, T = (128, 64, 512)
        Bn = x.shape[0]
        Fn = amplitudes.shape[0]
        a = amplitudes[None, :] ** delta_t[:, None]
        ang = frequencies[None, :] * delta_t[:, None]
        c = a * jnp.cos(ang)
        s = a * jnp.sin(ang)
        xr = x.reshape(Bn, Fn, 2, -1)
        x0, x1 = (xr[:, :, 0], xr[:, :, 1])
        out0 = c[..., None] * x0 - s[..., None] * x1
        out1 = s[..., None] * x0 + c[..., None] * x1
        return jnp.stack([out0, out1], axis=2).reshape(x.shape)

    def _L2_cond_ref(x, cat_ids, W, b):
        import jax, jax.numpy as jnp
        import numpy as np
        NUM_CATEGORIES = 64
        INPUT_DIM = 512
        HIDDEN_DIM = 512
        B = 128
        S = 64
        selected_W = W[cat_ids]
        selected_b = b[cat_ids]
        out = jnp.einsum('bsd,bdh->bsh', x, selected_W) + selected_b[:, None, :]
        return out

    def _L3_cond_ref(hidden_states, language_ids, W1, b1, W2, b2, gamma, beta):
        import jax, jax.numpy as jnp
        import numpy as np
        LN_EPS = 1e-05
        w1 = W1[language_ids]
        w2 = W2[language_ids]
        h = jnp.einsum('bsh,bha->bsa', hidden_states, w1) + b1[language_ids][:, None, :]
        h = jax.nn.relu(h)
        adapted = jnp.einsum('bsa,bah->bsh', h, w2) + b2[language_ids][:, None, :]
        x = hidden_states + adapted
        mean = jnp.mean(x, axis=-1, keepdims=True)
        var = jnp.mean(jnp.square(x - mean), axis=-1, keepdims=True)
        normed = (x - mean) * jax.lax.rsqrt(var + LN_EPS)
        return normed * gamma[language_ids][:, None, :] + beta[language_ids][:, None, :]
    x = x + _L0_cond_ref(x, itok_B_0_7, L0_cond_weight, L0_cond_bias)
    x = x + _L1_cond_ref(x, condB_deltat, L1_cond_amplitudes, L1_cond_frequencies)
    x = x + _L2_cond_ref(x, itok_B_0_63, L2_cond_W, L2_cond_b)
    x = x + _L3_cond_ref(x, itok_B_0_8, L3_cond_W1, L3_cond_b1, L3_cond_W2, L3_cond_b2, L3_cond_gamma, L3_cond_beta)
    return x

_drawn_inputs = setup_inputs


def setup_inputs(seed=0):
    import zlib

    import numpy as np

    out = dict(_drawn_inputs(seed))
    spreads = {'L2_cond_b': (0.0, 0.1),
     'L3_cond_b1': (0.0, 0.331),
     'L3_cond_b2': (0.0, 0.1),
     'L3_cond_gamma': (1.0, 0.2),
     'L3_cond_beta': (0.0, 0.1)}
    factors = {}
    for name, (base, spread) in spreads.items():
        noise = np.random.default_rng([zlib.crc32(name.encode()), seed]).standard_normal(out[name].shape)
        drawn = base * np.exp(spread * noise) if base else spread * noise
        out[name] = jnp.asarray(drawn.astype(out[name].dtype))
    for name, factor in factors.items():
        out[name] = (out[name] * factor).astype(out[name].dtype)
    return out
```

```python
import concourse.bass as bass
from concourse import mybir
from contextlib import ExitStack

fp32 = mybir.dt.float32
i32 = mybir.dt.int32
ALU = mybir.AluOpType
ACT = mybir.ActivationFunctionType

LN_EPS = 1e-5
PI = 3.14159265358979
PI_BELOW = 3.1415925
TWO_PI = (6.28125, 1.9350051879882812e-3, 3.0199159819388e-7)
ROUND = 12582912.0


def conditioned_residual_stack(
    nc: bass.Bass,
    xT: bass.AP,
    subject: bass.AP,
    category: bass.AP,
    language: bass.AP,
    delta_t: bass.AP,
    W0T: bass.AP,
    b0: bass.AP,
    amp_tok: bass.AP,
    freq_tok: bass.AP,
    W2: bass.AP,
    b2: bass.AP,
    W1: bass.AP,
    b1T: bass.AP,
    Wup: bass.AP,
    bup: bass.AP,
    gamma: bass.AP,
    beta: bass.AP,
    out: bass.AP,
):
    B, P, C, N = xT.shape
    S, D = b0.shape
    K = b2.shape[0]
    L, A = b1T.shape[1], b1T.shape[0]
    U = 4
    YB = 4
    LAST = B - 1

    ctx = ExitStack()
    with ctx:
        def sb(name, shape, dt=fp32):
            return ctx.enter_context(nc.sbuf_tensor(name, shape, dt))

        def pb(name, shape):
            return ctx.enter_context(nc.psum_tensor(name, shape, fp32))

        def sem(name):
            return ctx.enter_context(nc.semaphore(name))

        w0_sb = sb("w0_sb", [P, S * C * D])
        w1_sb = sb("w1_sb", [P, L * C * A])
        wup_sb = sb("wup_sb", [A, L * D])
        b0_sb = sb("b0_sb", [P, S * D])
        gamma_sb = sb("gamma_sb", [P, L * D])
        beta_sb = sb("beta_sb", [P, L * D])
        b1_sb = sb("b1_sb", [A, L])
        ids = sb("ids", [1, 3 * B], i32)
        ident = sb("ident", [P, P])
        signed_swap = sb("signed_swap", [N, N])
        cos1 = sb("cos1", [N, B])
        sin1 = sb("sin1", [N, B])
        x_in = [sb(f"x_in{i}", [P, C * N]) for i in range(2)]
        w2_in = [sb(f"w2_in{i}", [P, C * D]) for i in range(2)]
        b2_in = [sb(f"b2_in{i}", [P, D]) for i in range(2)]
        x1 = sb("x1", [N, D])
        diag = sb("diag", [N, N])
        mix = [sb(f"mix{i}", [N, N]) for i in range(2)]
        x2T = sb("x2T", [P, C * N])
        x3 = [sb(f"x3_{i}", [N, D]) for i in range(2)]
        x3beta = [sb(f"x3beta{i}", [N, D]) for i in range(2)]
        x3T = sb("x3T", [P, C * N])
        h = sb("h", [N, A])
        hT = [sb(f"hT{i}", [A, N]) for i in range(2)]
        yb = [sb(f"yb{i}", [N, D]) for i in range(YB)]
        stats = sb("stats", [N, 6])
        mean_var = sb("mean_var", [N, 2])
        var_eps = sb("var_eps", [N, 1])
        eps = sb("eps", [N, 1])
        minus_half = sb("minus_half", [N, 1])
        rstd = sb("rstd", [N, 1])
        dt_sb = x1[:, 0:B]
        ang = x1[:, B:2 * B]
        turns = x1[:, 2 * B:3 * B]
        angle_sin = x1[:, 3 * B:4 * B]
        angle_cos = x3[0][:, 0:B]
        power = x3[0][:, B:2 * B]
        sine = x3[0][:, 2 * B:3 * B]
        cosine = x3[0][:, 3 * B:4 * B]
        cols = stats[:, 0:2]

        ps_l0 = pb("ps_l0", [N, D])
        ps_mix = pb("ps_mix", [P, C * N])
        ps_l2 = pb("ps_l2", [N, D])
        ps_x3T = pb("ps_x3T", [P, C * N])
        ps_h = pb("ps_h", [N, A])
        ps_hT = pb("ps_hT", [A, N])
        ps_up = pb("ps_up", [N, D])

        ids_loaded = sem("ids_loaded")
        small_loaded = sem("small_loaded")
        w0_loaded = sem("w0_loaded")
        b0_loaded = sem("b0_loaded")
        l3_loaded = sem("l3_loaded")
        x_loaded = [sem(f"x_loaded{i}") for i in range(2)]
        w2_loaded = [sem(f"w2_loaded{i}") for i in range(2)]
        b2_loaded = [sem(f"b2_loaded{i}") for i in range(2)]
        yb_loaded = [sem(f"yb_loaded{i}") for i in range(YB)]
        out_stored = [sem(f"out_stored{i}") for i in range(YB)]
        zeroed = sem("zeroed")
        consts_made = sem("consts_made")
        w0_folded = sem("w0_folded")
        power_made = sem("power_made")
        chained = sem("chained")
        angles_reduced = sem("angles_reduced")
        trig_made = sem("trig_made")
        coef_made = sem("coef_made")
        l0_done = sem("l0_done")
        mix_done = sem("mix_done")
        l2_done = sem("l2_done")
        x3T_done = sem("x3T_done")
        h_done = sem("h_done")
        hT_done = sem("hT_done")
        up_done = sem("up_done")
        x1_made = sem("x1_made")
        diag_made = sem("diag_made")
        mix_made = sem("mix_made")
        x2T_made = sem("x2T_made")
        w2_folded = sem("w2_folded")
        x3_made = sem("x3_made")
        x3T_made = sem("x3T_made")
        h_made = sem("h_made")
        hT_made = sem("hT_made")
        x3bias_made = sem("x3bias_made")
        x3beta_made = sem("x3beta_made")
        y_made = sem("y_made")
        stats_made = sem("stats_made")
        mean_made = sem("mean_made")
        var_eps_made = sem("var_eps_made")
        rstd_made = sem("rstd_made")
        scaled_made = sem("scaled_made")
        out_made = sem("out_made")

        block = ctx.enter_context(nc.Block())

        def subject_of(eng, s):
            return eng.value_load(ids[0:1, bass.ds(s, 1)], min_val=0, max_val=S - 1)

        def category_of(eng, s):
            return eng.value_load(ids[0:1, bass.ds(B + s, 1)], min_val=0, max_val=K - 1)

        def language_of(eng, s):
            return eng.value_load(ids[0:1, bass.ds(2 * B + s, 1)], min_val=0, max_val=L - 1)

        def diagonal_of(tile):
            return bass.AP(tile[:, :].tensor, 0, [[C * D, P], [D + P, C], [1, P]])

        def over_samples(eng, step):
            for s in range(U):
                step(s, s, s)
            with nc.Fori(U, B - U, U, engines=[eng.engine]) as i:
                for j in range(U):
                    step(i + j, U, j)
            for j in range(U):
                step(B - U + j, B - U + j, j)

        @block.sync
        def _(sp):
            for n, row in enumerate((subject, category, language)):
                sp.dma_start(ids[0:1, n * B:(n + 1) * B], row).then_inc(ids_loaded, 16)
            sp.dma_start(dt_sb, delta_t.partition_broadcast(N)).then_inc(small_loaded, 16)
            sp.dma_start(cols[:, 0:1], amp_tok).then_inc(small_loaded, 16)
            sp.dma_start(cols[:, 1:2], freq_tok).then_inc(small_loaded, 16)
            sp.dma_start(x_in[0][:, :], xT[0].rearrange("p c n -> p (c n)")).then_inc(x_loaded[0], 16)
            sp.dma_start(b0_sb[:, :], b0.rearrange("s d -> (s d)").partition_broadcast(P)).then_inc(b0_loaded, 16)
            sp.dma_start(w0_sb[:, :], W0T.rearrange("p s c d -> p (s c d)")).then_inc(w0_loaded, 16)
            sp.wait_ge(ids_loaded, 48)

            def step(s, k, j):
                cat = category_of(sp, s)
                if k >= 2:
                    sp.wait_ge(l2_done, s - 1)
                sp.dma_start(w2_in[j % 2][:, :], W2[bass.ds(cat, 1)].rearrange("o p c d -> p (o c d)"))\
                    .then_inc(w2_loaded[j % 2], 16)
                if k >= 2:
                    sp.wait_ge(x3_made, s - 1)
                sp.dma_start(b2_in[j % 2][:, :], b2[bass.ds(cat, 1)].rearrange("o d -> (o d)").partition_broadcast(P))\
                    .then_inc(b2_loaded[j % 2], 16)
                if k == 0:
                    for dst, src in ((w1_sb, W1.rearrange("p l c a -> p (l c a)")),
                                     (wup_sb, Wup.rearrange("p l d -> p (l d)")),
                                     (b1_sb, b1T),
                                     (gamma_sb, gamma.rearrange("l d -> (l d)").partition_broadcast(P)),
                                     (beta_sb, beta.rearrange("l d -> (l d)").partition_broadcast(P))):
                        sp.dma_start(dst[:, :], src).then_inc(l3_loaded, 16)
                if k >= YB:
                    sp.wait_ge(out_made, s - YB + 1)
                    sp.dma_start(out[bass.ds(s - YB, 1)].rearrange("o n d -> n (o d)"), yb[j % YB][:, :])\
                        .then_inc(out_stored[j % YB], 16)
                if k < LAST:
                    if k >= 1:
                        sp.wait_ge(l0_done, s)
                    sp.dma_start(x_in[(j + 1) % 2][:, :], xT[bass.ds(s + 1, 1)].rearrange("o p c n -> p (o c n)"))\
                        .then_inc(x_loaded[(j + 1) % 2], 16)
                lang = language_of(sp, s)
                if k >= YB:
                    sp.wait_ge(out_stored[j % YB], (s - j) * (16 // YB))
                sp.dma_start(yb[j % YB][:, :], bup[bass.ds(lang, 1)].rearrange("o d -> (o d)").partition_broadcast(P))\
                    .then_inc(yb_loaded[j % YB], 16)

            over_samples(sp, step)
            for s in range(B - YB, B):
                sp.wait_ge(out_made, s + 1)
                sp.dma_start(out[s], yb[s % YB][:, :]).then_inc(out_stored[s % YB], 16)
            for b in range(YB):
                sp.wait_ge(out_stored[b], 16 * (B // YB))

        @block.gpsimd
        def _(pool):
            pool.memset(ident[:, :], 0.0).then_inc(zeroed, 1)
            pool.memset(signed_swap[:, :], 0.0).then_inc(zeroed, 1)
            pool.memset(minus_half[:, :], -0.5).then_inc(zeroed, 1)
            pool.memset(eps[:, :], LN_EPS).then_inc(zeroed, 1)
            pool.wait_ge(zeroed, 4)
            pool.affine_select(out=ident[:, :], in_=ident[:, :], compare_op=ALU.not_equal, fill=1.0,
                               base=0, pattern=[[-1, P]], channel_multiplier=1).then_inc(consts_made, 1)
            pairs = signed_swap[:, :].rearrange("p (f e) -> p e f", e=2)
            pool.affine_select(out=pairs[:, 1], in_=pairs[:, 1], compare_op=ALU.not_equal, fill=1.0,
                               base=0, pattern=[[-2, N // 2]], channel_multiplier=1).then_inc(consts_made, 1)
            pool.affine_select(out=pairs[:, 0], in_=pairs[:, 0], compare_op=ALU.not_equal, fill=-1.0,
                               base=-1, pattern=[[-2, N // 2]], channel_multiplier=1).then_inc(consts_made, 1)
            pool.wait_ge(small_loaded, 48)
            pool.tensor_tensor(power, cols[:, 0:1].broadcast_to([N, B]), dt_sb, ALU.pow).then_inc(power_made, 1)
            pool.wait_ge(consts_made, 3)
            w0_v = w0_sb[:, :].rearrange("p (s c d) -> p s c d", s=S, c=C)
            for c in range(C):
                blk = w0_v[:, :, c, c * P:(c + 1) * P]
                if c == 0:
                    pool.wait_ge(w0_loaded, 16)
                pool.tensor_tensor(blk, blk, ident[:, :].unsqueeze(1).broadcast_to([P, S, P]), ALU.add)\
                    .then_inc(w0_folded, 1)
            pool.wait_ge(l3_loaded, 80)

            def fold(s, k, j):
                diagonal = diagonal_of(w2_in[j % 2])
                pool.wait_ge(w2_loaded[j % 2], (s - j) * 8 + 16 * (j // 2) + 16)
                pool.tensor_tensor(diagonal, diagonal, ident[:, :].unsqueeze(1).broadcast_to([P, C, P]), ALU.add)\
                    .then_inc(w2_folded, 1)

            def inverse_deviation(s):
                pool.wait_ge(mean_made, s + 1)
                pool.tensor_tensor(var_eps[:, :], mean_var[:, 1:2], eps[:, :], ALU.add).then_inc(var_eps_made, 1)
                pool.wait_ge(var_eps_made, s + 1)
                pool.tensor_tensor(rstd[:, :], var_eps[:, :], minus_half[:, :], ALU.pow).then_inc(rstd_made, 1)

            fold(0, 0, 0)

            def step(s, k, j):
                if k < LAST:
                    fold(s + 1, k + 1, j + 1)
                lang = language_of(pool, s)
                pool.wait_ge(yb_loaded[j % YB], (s - j) * (16 // YB) + 16)
                pool.wait_ge(x3_made, s + 1)
                pool.tensor_tensor(yb[j % YB][:, :], x3[j % 2][:, :], yb[j % YB][:, :], ALU.add)\
                    .then_inc(x3bias_made, 1)
                if k >= 2:
                    pool.wait_ge(out_made, s - 1)
                pool.tensor_tensor(x3beta[j % 2][:, :], x3[j % 2][:, :], beta_sb[:, bass.ds(lang * D, D)], ALU.add)\
                    .then_inc(x3beta_made, 1)

                if k >= 1:
                    inverse_deviation(s - 1)

            over_samples(pool, step)
            inverse_deviation(LAST)

        @block.scalar
        def _(act):
            act.wait_ge(angles_reduced, 1)
            act.activation(sine, angle_sin, ACT.Sin).then_inc(trig_made, 1)
            act.wait_ge(angles_reduced, 2)
            act.activation(cosine, angle_cos, ACT.Sin).then_inc(trig_made, 1)
            act.wait_ge(coef_made, 2)
            act.wait_ge(consts_made, 3)
            act.wait_ge(l3_loaded, 80)

            def make_diag(s, k):
                if k >= 1:
                    act.wait_ge(mix_made, s)
                act.activation(diag[:, :], ident[:, :], ACT.Copy, scale=cos1[:, bass.ds(s, 1)])\
                    .then_inc(diag_made, 1)

            def evacuate_mix(s, k):
                act.wait_ge(mix_done, s + 1)
                if k >= 1:
                    act.wait_ge(l2_done, s)
                act.activation(x2T[:, :], ps_mix[:, :], ACT.Copy).then_inc(x2T_made, 1)

            make_diag(0, 0)
            evacuate_mix(0, 0)

            def step(s, k, j):
                if k < LAST:
                    make_diag(s + 1, k + 1)
                act.wait_ge(x3T_done, s + 1)
                if k >= 1:
                    act.wait_ge(h_done, s)
                act.activation(x3T[:, :], ps_x3T[:, :], ACT.Copy).then_inc(x3T_made, 1)
                if k < LAST:
                    evacuate_mix(s + 1, k + 1)
                lang = language_of(act, s)
                act.wait_ge(hT_done, s + 1)
                if k >= 2:
                    act.wait_ge(up_done, s - 1)
                act.activation(hT[j % 2][:, :], ps_hT[:, :], ACT.Relu, bias=b1_sb[:, bass.ds(lang, 1)])\
                    .then_inc(hT_made, 1)

            over_samples(act, step)

        @block.vector
        def _(dve):
            chain = [0]

            def link(ins):
                chain[0] += 1
                ins.then_inc(chained, 1)
                dve.wait_ge(chained, chain[0])

            dve.wait_ge(small_loaded, 48)
            link(dve.tensor_scalar(ang, dt_sb, cols[:, 1:2], None, ALU.mult))
            for red, shift in ((angle_sin, 0.0), (angle_cos, 0.25)):
                link(dve.tensor_scalar(turns, ang, 0.5 / PI, shift, ALU.mult, ALU.add))
                link(dve.tensor_scalar(turns, turns, ROUND, None, ALU.add))
                link(dve.tensor_scalar(turns, turns, ROUND, None, ALU.subtract))
                link(dve.scalar_tensor_tensor(out=red, in0=turns, scalar=-TWO_PI[0], in1=ang,
                                              op0=ALU.mult, op1=ALU.add))
                for part in TWO_PI[1:]:
                    link(dve.scalar_tensor_tensor(out=red, in0=turns, scalar=-part, in1=red,
                                                  op0=ALU.mult, op1=ALU.add))
                link(dve.tensor_scalar(red, red, shift * 2 * PI, None, ALU.add))
                dve.tensor_scalar(red, red, PI_BELOW, -PI_BELOW, ALU.min, ALU.max).then_inc(angles_reduced, 1)
            dve.wait_ge(power_made, 1)
            dve.wait_ge(trig_made, 2)
            dve.tensor_tensor(sin1[:, :], power, sine, ALU.mult).then_inc(coef_made, 1)
            link(dve.tensor_tensor(cosine, power, cosine, ALU.mult))
            dve.tensor_scalar(cos1[:, :], cosine, 1.0, None, ALU.add).then_inc(coef_made, 1)
            dve.wait_ge(coef_made, 2)
            dve.wait_ge(consts_made, 3)
            dve.wait_ge(b0_loaded, 16)
            dve.wait_ge(l3_loaded, 80)

            def make_mix(s, k, j):
                dve.wait_ge(diag_made, s + 1)
                if k >= 2:
                    dve.wait_ge(mix_done, s - 1)
                dve.scalar_tensor_tensor(out=mix[j % 2][:, :], in0=signed_swap[:, :], scalar=sin1[:, bass.ds(s, 1)],
                                         in1=diag[:, :], op0=ALU.mult, op1=ALU.add).then_inc(mix_made, 1)

            def finish_l0(s, k):
                sub = subject_of(dve, s)
                dve.wait_ge(l0_done, s + 1)
                if k >= 1:
                    dve.wait_ge(mix_done, s)
                dve.tensor_tensor(x1[:, :], ps_l0[:, :], b0_sb[:, bass.ds(sub * D, D)], ALU.add).then_inc(x1_made, 1)

            def finish_l2(s, k, j):
                dve.wait_ge(b2_loaded[j % 2], (s - j) * 8 + 16 * (j // 2) + 16)
                dve.wait_ge(l2_done, s + 1)
                if k >= 2:
                    dve.wait_ge(x3T_done, s - 1)
                    dve.wait_ge(x3beta_made, s - 1)
                dve.tensor_tensor(x3[j % 2][:, :], ps_l2[:, :], b2_in[j % 2][:, :], ALU.add).then_inc(x3_made, 1)

            def finish_h(s, k):
                dve.wait_ge(h_done, s + 1)
                if k >= 1:
                    dve.wait_ge(hT_done, s)
                dve.tensor_copy(h[:, :], ps_h[:, :]).then_inc(h_made, 1)

            def normalise(s, j):
                lang = language_of(dve, s)
                y = yb[j % YB]
                dve.wait_ge(up_done, s + 1)
                dve.wait_ge(x3bias_made, s + 1)
                dve.tensor_tensor(y[:, :], ps_up[:, :], y[:, :], ALU.add).then_inc(y_made, 1)
                dve.wait_ge(y_made, s + 1)
                dve.bn_stats(stats[:, :], y[:, :]).then_inc(stats_made, 1)
                dve.wait_ge(coef_made, 2)
                dve.wait_ge(stats_made, s + 1)
                dve.bn_aggr(mean_var[:, :], stats[:, :]).then_inc(mean_made, 1)
                dve.wait_ge(mean_made, s + 1)
                dve.scalar_tensor_tensor(out=y[:, :], in0=y[:, :], scalar=mean_var[:, 0:1],
                                         in1=gamma_sb[:, bass.ds(lang * D, D)],
                                         op0=ALU.subtract, op1=ALU.mult).then_inc(scaled_made, 1)
                dve.wait_ge(rstd_made, s + 1)
                dve.wait_ge(scaled_made, s + 1)
                dve.wait_ge(x3beta_made, s + 1)
                dve.scalar_tensor_tensor(out=y[:, :], in0=y[:, :], scalar=rstd[:, 0:1], in1=x3beta[j % 2][:, :],
                                         op0=ALU.mult, op1=ALU.add).then_inc(out_made, 1)

            make_mix(0, 0, 0)
            finish_l0(0, 0)

            def step(s, k, j):
                finish_l2(s, k, j)
                if k < LAST:
                    make_mix(s + 1, k + 1, j + 1)
                    finish_l0(s + 1, k + 1)
                finish_h(s, k)
                if k >= 1:
                    normalise(s - 1, j - 1)

            over_samples(dve, step)
            normalise(LAST, LAST)

        @block.tensor
        def _(pe):
            def l0(s, k, j, sub, chunks):
                if chunks[0] == 0:
                    pe.wait_ge(x_loaded[j % 2], (s - j) * 8 + 16 * (j // 2) + 16)
                    if k >= 1:
                        pe.wait_ge(x1_made, s)
                for c in chunks:
                    mm = pe.matmul(ps_l0[:, :], x_in[j % 2][:, c * N:(c + 1) * N],
                                   w0_sb[:, bass.ds(sub * (C * D) + c * D, D)], start=(c == 0), stop=(c == C - 1))
                if chunks[-1] == C - 1:
                    mm.then_inc(l0_done, 1)

            def rotate(s, k, j):
                pe.wait_ge(x1_made, s + 1)
                pe.wait_ge(mix_made, s + 1)
                if k >= 1:
                    pe.wait_ge(x2T_made, s)
                for c in range(C):
                    mm = pe.matmul(ps_mix[:, c * N:(c + 1) * N], x1[:, c * P:(c + 1) * P], mix[j % 2][:, :],
                                   start=True, stop=True)
                mm.then_inc(mix_done, 1)

            def l2(s, k, j):
                pe.wait_ge(x2T_made, s + 1)
                pe.wait_ge(w2_folded, s + 1)
                if k >= 1:
                    pe.wait_ge(x3_made, s)
                for c in range(C):
                    mm = pe.matmul(ps_l2[:, :], x2T[:, c * N:(c + 1) * N], w2_in[j % 2][:, c * D:(c + 1) * D],
                                   start=(c == 0), stop=(c == C - 1))
                mm.then_inc(l2_done, 1)

            def transpose_x3(s, k, j):
                pe.wait_ge(x3_made, s + 1)
                if k >= 1:
                    pe.wait_ge(x3T_made, s)
                for c in range(C):
                    mm = pe.transpose(ps_x3T[:, c * N:(c + 1) * N], x3[j % 2][:, c * P:(c + 1) * P], ident[:, :])
                mm.then_inc(x3T_done, 1)

            def down(s, k, lang):
                pe.wait_ge(x3T_made, s + 1)
                if k >= 1:
                    pe.wait_ge(h_made, s)
                for c in range(C):
                    mm = pe.matmul(ps_h[:, :], x3T[:, c * N:(c + 1) * N],
                                   w1_sb[:, bass.ds(lang * (C * A) + c * A, A)], start=(c == 0), stop=(c == C - 1))
                mm.then_inc(h_done, 1)

            def transpose_h(s, k):
                pe.wait_ge(h_made, s + 1)
                if k >= 1:
                    pe.wait_ge(hT_made, s)
                pe.transpose(ps_hT[:, :], h[:, :], ident[:, :]).then_inc(hT_done, 1)

            def up(s, k, j, lang):
                pe.wait_ge(hT_made, s + 1)
                if k >= 1:
                    pe.wait_ge(y_made, s)
                pe.matmul(ps_up[:, :], hT[j % 2][:, :], wup_sb[:, bass.ds(lang * D, D)], start=True, stop=True)\
                    .then_inc(up_done, 1)

            pe.wait_ge(ids_loaded, 48)
            pe.wait_ge(w0_folded, C)
            pe.wait_ge(consts_made, 3)
            l0(0, 0, 0, subject_of(pe, 0), range(C))
            rotate(0, 0, 0)
            l2(0, 0, 0)
            pe.wait_ge(l3_loaded, 80)

            def step(s, k, j):
                if k < LAST:
                    sub = subject_of(pe, s + 1)
                    l0(s + 1, k + 1, j + 1, sub, range(0, C // 2))
                transpose_x3(s, k, j)
                if k < LAST:
                    l0(s + 1, k + 1, j + 1, sub, range(C // 2, C))
                lang = language_of(pe, s)
                down(s, k, lang)
                if k < LAST:
                    rotate(s + 1, k + 1, j + 1)
                transpose_h(s, k)
                if k >= 1:
                    up(s - 1, k - 1, j - 1, language_of(pe, s - 1))
                if k < LAST:
                    l2(s + 1, k + 1, j + 1)

            over_samples(pe, step)
            up(LAST, LAST, LAST, language_of(pe, LAST))


def kernel(**inputs):
    import numpy as _np
    import concourse.bacc as _bacc
    from concourse import mybir as _mybir
    from concourse.bass_utils import run_bass_kernel_spmd as _run

    a = {name: _np.asarray(v) for name, v in inputs.items()}
    x = a["x"]
    B, N, D = x.shape
    P = 128
    C = D // P

    def feature_major(w):
        n, _, cols = w.shape
        return w.reshape(n, C, P, cols).transpose(0, 2, 1, 3)

    arrays = {
        "xT": feature_major(x.transpose(0, 2, 1)),
        "subject": a["itok_B_0_7"].reshape(1, B),
        "category": a["itok_B_0_63"].reshape(1, B),
        "language": a["itok_B_0_8"].reshape(1, B),
        "delta_t": a["condB_deltat"].reshape(1, B),
        "W0T": feature_major(a["L0_cond_weight"].transpose(0, 2, 1)).transpose(1, 0, 2, 3),
        "b0": a["L0_cond_bias"],
        "amp_tok": _np.repeat(a["L1_cond_amplitudes"], 2).reshape(N, 1),
        "freq_tok": _np.repeat(a["L1_cond_frequencies"], 2).reshape(N, 1),
        "W2": feature_major(a["L2_cond_W"]),
        "b2": a["L2_cond_b"],
        "W1": feature_major(a["L3_cond_W1"]).transpose(1, 0, 2, 3),
        "b1T": a["L3_cond_b1"].transpose(1, 0),
        "Wup": a["L3_cond_W2"].transpose(1, 0, 2),
        "bup": a["L3_cond_b2"],
        "gamma": a["L3_cond_gamma"],
        "beta": a["L3_cond_beta"],
    }
    nc = _bacc.Bacc("TRN2", target_bir_lowering=False, num_devices=1,
                     dynamic_dma_scratch_size=1024)
    args = []
    for name in arrays:
        arrays[name] = _np.ascontiguousarray(arrays[name])
        args.append(nc.dram_tensor(name, arrays[name].shape, _mybir.dt.from_np(arrays[name].dtype),
                                   kind="ExternalInput").ap())
    args.append(nc.dram_tensor("out", (B, N, D), fp32, kind="ExternalOutput").ap())
    conditioned_residual_stack(nc, *args)
    r = _run(nc, [arrays], core_ids=[0])
    return r.results[0]["out"]
```

```python
import concourse.bass as bass
from concourse import mybir
from contextlib import ExitStack

fp32 = mybir.dt.float32
fp32r = mybir.dt.float32r
i32 = mybir.dt.int32
ALU = mybir.AluOpType
ACT = mybir.ActivationFunctionType

LN_EPS = 1e-5
PI = 3.14159265358979
PI_BELOW = 3.1415925
TWO_PI = (6.28125, 1.9350051879882812e-3, 3.0199159819388e-7)
ROUND = 12582912.0


def conditioned_residual_stack(
    nc: bass.Bass,
    xT: bass.AP,
    subject: bass.AP,
    category: bass.AP,
    language: bass.AP,
    delta_t: bass.AP,
    W0T: bass.AP,
    b0: bass.AP,
    amp_tok: bass.AP,
    freq_tok: bass.AP,
    W2: bass.AP,
    b2: bass.AP,
    W1: bass.AP,
    b1T: bass.AP,
    Wup: bass.AP,
    bup: bass.AP,
    gamma: bass.AP,
    beta: bass.AP,
    out: bass.AP,
):
    B, P, C, N = xT.shape
    S, D = b0.shape
    K = b2.shape[0]
    L, A = b1T.shape[1], b1T.shape[0]
    U = 4
    SOON, LATER = 2 * U, B // 4
    YB = 4
    XB = 4
    LAST = B - 1
    WD = C * D

    ctx = ExitStack()
    with ctx:
        def sb(name, shape, dt=fp32):
            return ctx.enter_context(nc.sbuf_tensor(name, shape, dt))

        def pb(name, shape):
            return ctx.enter_context(nc.psum_tensor(name, shape, fp32))

        def sem(name):
            return ctx.enter_context(nc.semaphore(name))

        w1_sb = sb("w1_sb", [P, L * C * A])
        wup_sb = sb("wup_sb", [A, L * D])
        bup_sb = sb("bup_sb", [P, L * D])
        gamma_sb = sb("gamma_sb", [P, L * D])
        beta_sb = sb("beta_sb", [P, L * D])
        b1_sb = sb("b1_sb", [A, L])
        ident = sb("ident", [P, P])
        signed_swap = sb("signed_swap", [N, N])
        ids = sb("ids", [1, 5 * B], i32)
        cos1 = sb("cos1", [N, B])
        sin1 = sb("sin1", [N, B])
        eps = sb("eps", [N, 1])
        minus_half = sb("minus_half", [N, 1])
        w0_in = sb("w0_in", [P, WD])
        b0_in = sb("b0_in", [P, D])
        w0_hi = sb("w0_hi", [P, WD], fp32r)
        w0_lo = sb("w0_lo", [P, WD], fp32r)
        b0_sb = sb("b0_sb", [P, D])
        x_in = [sb(f"x_in{i}", [P, C * N]) for i in range(XB)]
        x_hi = sb("x_hi", [P, C * N], fp32r)
        x_lo = sb("x_lo", [P, C * N], fp32r)
        w2_in = [sb(f"w2_in{i}", [P, WD]) for i in range(2)]
        w2_hi = sb("w2_hi", [P, WD], fp32r)
        w2_lo = sb("w2_lo", [P, WD], fp32r)
        b2_in = [sb(f"b2_in{i}", [P, D]) for i in range(2)]
        x1 = sb("x1", [N, D])
        diag = sb("diag", [N, N])
        mix = sb("mix", [N, N])
        x2T_hi = sb("x2T_hi", [P, C * N], fp32r)
        x2T_lo = sb("x2T_lo", [P, C * N], fp32r)
        x3 = [sb(f"x3_{i}", [N, D]) for i in range(YB)]
        x3T = sb("x3T", [P, C * N])
        h = sb("h", [N, A])
        hT = sb("hT", [A, N])
        yb = [sb(f"yb{i}", [N, D]) for i in range(YB)]
        stats = sb("stats", [N, 6])
        mean_var = sb("mean_var", [N, 2])
        var_eps = sb("var_eps", [N, 1])
        rstd = sb("rstd", [N, 1])

        ps_l0 = pb("ps_l0", [N, D])
        ps_mix = pb("ps_mix", [P, C * N])
        ps_l2 = pb("ps_l2", [N, D])
        ps_x3T = pb("ps_x3T", [P, C * N])
        ps_h = pb("ps_h", [N, A])
        ps_hT = pb("ps_hT", [A, N])
        ps_up = pb("ps_up", [N, D])

        def column(n):
            return stats_cols[:, n:n + 1]

        stats_cols = sb("stats_cols", [P, 16])
        icols = stats_cols[:, 8:12].bitcast(i32)
        cols = stats_cols[:, 0:5]
        dt_col, amp_col, freq_col = (stats_cols[:, n:n + 1] for n in (5, 6, 7))
        key_col, rank = (stats_cols[:, n:n + 1] for n in (12, 13))
        irows = x3[0][:, 0:2 * B].bitcast(i32)
        place_row = x3[0][:, 2 * B:3 * B]
        subject_row = x3[0][:, 3 * B:4 * B]
        key_row = x3T[:, 0:B]
        compared = x3T[:, B:2 * B]
        same = x3T[:, 2 * B:3 * B]
        dt_wide = x3T[:, 3 * B:4 * B]
        onehot = h[:, :]
        ang, turns, angle_sin, angle_cos = (x1[:, n * B:(n + 1) * B] for n in range(4))
        dt_sb, power, sine, cosine = (x3[YB - 1][:, n * B:(n + 1) * B] for n in range(4))

        small_loaded = sem("small_loaded")
        w1_loaded = sem("w1_loaded")
        bup_loaded = sem("bup_loaded")
        wup_loaded = sem("wup_loaded")
        beta_loaded = sem("beta_loaded")
        gamma_loaded = sem("gamma_loaded")
        w0_loaded = sem("w0_loaded")
        x_loaded = [sem(f"x_loaded{i}") for i in range(XB)]
        w2_loaded = [sem(f"w2_loaded{i}") for i in range(2)]
        b2_loaded = [sem(f"b2_loaded{i}") for i in range(2)]
        out_stored = [sem(f"out_stored{i}") for i in range(YB)]
        zeroed = sem("zeroed")
        consts_made = sem("consts_made")
        places_made = sem("places_made")
        onehot_made = sem("onehot_made")
        sorted_done = sem("sorted_done")
        ids_made = sem("ids_made")
        dt_made = sem("dt_made")
        power_made = sem("power_made")
        chained = sem("chained")
        angles_reduced = sem("angles_reduced")
        trig_made = sem("trig_made")
        coef_made = sem("coef_made")
        w0_folded = sem("w0_folded")
        w0_hi_made = sem("w0_hi_made")
        w0_lo_made = sem("w0_lo_made")
        b0_made = sem("b0_made")
        x_hi_made = sem("x_hi_made")
        x_lo_made = sem("x_lo_made")
        l0_done = sem("l0_done")
        mix_done = sem("mix_done")
        l2_done = sem("l2_done")
        x3T_done = sem("x3T_done")
        h_done = sem("h_done")
        hT_done = sem("hT_done")
        up_done = sem("up_done")
        x1_made = sem("x1_made")
        diag_made = sem("diag_made")
        mix_made = sem("mix_made")
        x2T_hi_made = sem("x2T_hi_made")
        x2T_lo_made = sem("x2T_lo_made")
        w2_folded = sem("w2_folded")
        w2_hi_made = sem("w2_hi_made")
        w2_lo_made = sem("w2_lo_made")
        x3_made = sem("x3_made")
        x3T_made = sem("x3T_made")
        h_made = sem("h_made")
        hT_made = sem("hT_made")
        x3bias_made = sem("x3bias_made")
        x3beta_made = sem("x3beta_made")
        y_made = sem("y_made")
        stats_made = sem("stats_made")
        mean_made = sem("mean_made")
        var_eps_made = sem("var_eps_made")
        rstd_made = sem("rstd_made")
        scaled_made = sem("scaled_made")
        out_made = sem("out_made")

        block = ctx.enter_context(nc.Block())

        def sample_of(eng, s):
            return eng.value_load(ids[0:1, bass.ds(s, 1)], min_val=0, max_val=B - 1)

        def subject_of(eng, s):
            return eng.value_load(ids[0:1, bass.ds(B + s, 1)], min_val=0, max_val=S - 1)

        def category_of(eng, s):
            return eng.value_load(ids[0:1, bass.ds(2 * B + s, 1)], min_val=0, max_val=K - 1)

        def language_of(eng, s):
            return eng.value_load(ids[0:1, bass.ds(3 * B + s, 1)], min_val=0, max_val=L - 1)

        def is_first(eng, s):
            return eng.value_load(ids[0:1, bass.ds(4 * B + s, 1)], min_val=0, max_val=1)

        def diagonal_of(tile):
            return bass.AP(tile[:, :].tensor, 0, [[WD, P], [D + P, C], [1, P]])

        def loads_of(j, s, n):
            return (s - j) * (16 // n) + 16 * (j // n) + 16

        halves = (slice(0, WD // 2), slice(WD // 2, WD))

        def over_samples(step):
            def run(eng):
                for s in range(U):
                    step(s, s, s)
                with nc.Fori(U, B - 2 * U + 1, U, engines=[eng.engine]) as i:
                    for j in range(U):
                        step(i + j, U, j)
                for j in range(U):
                    step(B - U + j, B - U + j, j)
            return run

        @block.sync
        def _(sp):
            sp.dma_start(irows[:, B:2 * B], subject.partition_broadcast(P)).then_inc(small_loaded, 16)
            for n, ids_dram in enumerate((subject, category, language)):
                sp.dma_start(icols[:, n + 1:n + 2], ids_dram.rearrange("a b -> b a")).then_inc(small_loaded, 16)
            sp.dma_start(dt_col, delta_t.rearrange("a b -> b a")).then_inc(small_loaded, 16)
            sp.dma_start(amp_col, amp_tok).then_inc(small_loaded, 16)
            sp.dma_start(freq_col, freq_tok).then_inc(small_loaded, 16)
            sp.dma_start(w1_sb[:, :], W1.rearrange("p l c a -> p (l c a)")).then_inc(w1_loaded, 16)
            sp.dma_start(bup_sb[:, :], bup.rearrange("l d -> (l d)").partition_broadcast(P)).then_inc(bup_loaded, 16)
            sp.wait_ge(ids_made, 2)

            def load_w0(s, k):
                if k == 0:
                    sub = subject_of(sp, s)
                    sp.dma_start(w0_in[:, :], W0T[bass.ds(sub, 1)].rearrange("o p c d -> p (o c d)")).then_inc(w0_loaded, 16)
                    sp.dma_start(b0_in[:, :], b0[bass.ds(sub, 1)].rearrange("o d -> (o d)").partition_broadcast(P))\
                        .then_inc(w0_loaded, 16)
                    return
                sp.wait_ge(w0_lo_made, 2 * s)
                sp.wait_ge(b0_made, s)
                first = is_first(sp, s)
                sub = subject_of(sp, s)
                with sp.If(first):
                    sp.dma_start(w0_in[:, :], W0T[bass.ds(sub, 1)].rearrange("o p c d -> p (o c d)")).then_inc(w0_loaded, 16)
                    sp.dma_start(b0_in[:, :], b0[bass.ds(sub, 1)].rearrange("o d -> (o d)").partition_broadcast(P))\
                        .then_inc(w0_loaded, 16)
                with sp.Else():
                    sp.sem_inc(w0_loaded, 32)

            def load_x(s, k, j):
                if k >= XB:
                    sp.wait_ge(x_lo_made, s - XB + 1)
                sp.dma_start(x_in[j % XB][:, :], xT[bass.ds(sample_of(sp, s), 1)].rearrange("o p c n -> p (o c n)"))\
                    .then_inc(x_loaded[j % XB], 16)

            def load_w2(s, k, j):
                cat = category_of(sp, s)
                if k >= 2:
                    sp.wait_ge(w2_lo_made, 2 * s - 2)
                sp.dma_start(w2_in[j % 2][:, :], W2[bass.ds(cat, 1)].rearrange("o p c d -> p (o c d)"))\
                    .then_inc(w2_loaded[j % 2], 16)

            def load_b2(s, k, j):
                cat = category_of(sp, s)
                if k >= 2:
                    sp.wait_ge(x3_made, s - 1)
                sp.dma_start(b2_in[j % 2][:, :], b2[bass.ds(cat, 1)].rearrange("o d -> (o d)").partition_broadcast(P))\
                    .then_inc(b2_loaded[j % 2], 16)

            def store_out(s, j):
                sample = sample_of(sp, s)
                sp.wait_ge(out_made, s + 1)
                sp.dma_start(out[bass.ds(sample, 1)].rearrange("o n d -> n (o d)"), yb[j % YB][:, :])\
                    .then_inc(out_stored[j % YB], 16)

            load_x(0, 0, 0)
            load_w0(0, 0)
            load_w2(0, 0, 0)
            load_b2(0, 0, 0)
            load_x(1, 1, 1)
            load_w2(1, 1, 1)
            load_b2(1, 1, 1)
            load_x(2, 2, 2)
            load_w0(1, 1)
            sp.dma_start(beta_sb[:, :], beta.rearrange("l d -> (l d)").partition_broadcast(P)).then_inc(beta_loaded, 16)
            sp.dma_start(wup_sb[:, :], Wup.rearrange("p l d -> p (l d)")).then_inc(wup_loaded, 16)
            sp.dma_start(b1_sb[:, :], b1T).then_inc(wup_loaded, 16)
            load_x(3, 3, 3)
            load_w0(2, 2)
            sp.dma_start(gamma_sb[:, :], gamma.rearrange("l d -> (l d)").partition_broadcast(P)).then_inc(gamma_loaded, 16)

            def step(s, k, j):
                if k < LAST - 1:
                    load_w2(s + 2, k + 2, j + 2)
                if k >= 2:
                    store_out(s - 2, j - 2)
                if k < LAST - 1:
                    load_b2(s + 2, k + 2, j + 2)
                if k < LAST - 3:
                    load_x(s + 4, k + 4, j + 4)
                if k < LAST - 2:
                    load_w0(s + 3, k + 3)

            over_samples(step)(sp)
            for s in range(B - 2, B):
                store_out(s, s)
            for b in range(YB):
                sp.wait_ge(out_stored[b], 16 * (B // YB))

        @block.gpsimd
        def _(pool):
            pool.iota(icols[:, 0:1], pattern=[[0, 1]], base=0, channel_multiplier=1).then_inc(places_made, 1)
            pool.iota(irows[:, 0:B], pattern=[[1, B]], base=0, channel_multiplier=0).then_inc(places_made, 1)
            pool.memset(ident[:, :], 0.0).then_inc(zeroed, 1)
            pool.memset(signed_swap[:, :], 0.0).then_inc(zeroed, 1)
            pool.memset(minus_half[:, :], -0.5).then_inc(zeroed, 1)
            pool.memset(eps[:, :], LN_EPS).then_inc(zeroed, 1)
            pool.wait_ge(zeroed, 4)
            pool.affine_select(out=ident[:, :], in_=ident[:, :], compare_op=ALU.not_equal, fill=1.0,
                               base=0, pattern=[[-1, P]], channel_multiplier=1).then_inc(consts_made, 1)
            pairs = signed_swap[:, :].rearrange("p (f e) -> p e f", e=2)
            pool.affine_select(out=pairs[:, 1], in_=pairs[:, 1], compare_op=ALU.not_equal, fill=1.0,
                               base=0, pattern=[[-2, N // 2]], channel_multiplier=1).then_inc(consts_made, 1)
            pool.affine_select(out=pairs[:, 0], in_=pairs[:, 0], compare_op=ALU.not_equal, fill=-1.0,
                               base=-1, pattern=[[-2, N // 2]], channel_multiplier=1).then_inc(consts_made, 1)
            pool.wait_ge(dt_made, 1)
            for places in (slice(0, SOON), slice(SOON, LATER)):
                pool.tensor_tensor(power[:, places], amp_col.broadcast_to([N, places.stop - places.start]),
                                   dt_sb[:, places], ALU.pow).then_inc(power_made, 1)
            pool.wait_ge(consts_made, 3)

            def fold_w0(s, k):
                pool.wait_ge(w0_loaded, 32 * s + 32)
                if k == 0:
                    pool.tensor_tensor(diagonal_of(w0_in), diagonal_of(w0_in),
                                       ident[:, :].unsqueeze(1).broadcast_to([P, C, P]), ALU.add).then_inc(w0_folded, 1)
                    return
                first = is_first(pool, s)
                with pool.If(first):
                    pool.tensor_tensor(diagonal_of(w0_in), diagonal_of(w0_in),
                                       ident[:, :].unsqueeze(1).broadcast_to([P, C, P]), ALU.add).then_inc(w0_folded, 1)
                with pool.Else():
                    pool.sem_inc(w0_folded, 1)

            def fold_w2(s, k, j):
                pool.wait_ge(w2_loaded[j % 2], loads_of(j, s, 2))
                pool.tensor_tensor(diagonal_of(w2_in[j % 2]), diagonal_of(w2_in[j % 2]),
                                   ident[:, :].unsqueeze(1).broadcast_to([P, C, P]), ALU.add).then_inc(w2_folded, 1)

            def rest_of_x(s, k, j):
                pool.wait_ge(x_hi_made, s + 1)
                if k >= 1:
                    pool.wait_ge(l0_done, s)
                pool.tensor_tensor(x_lo[:, :], x_in[j % XB][:, :], x_hi[:, :].bitcast(fp32), ALU.subtract).then_inc(x_lo_made, 1)

            def inverse_deviation(s):
                pool.wait_ge(mean_made, s + 1)
                pool.tensor_tensor(var_eps[:, :], mean_var[:, 1:2], eps[:, :], ALU.add).then_inc(var_eps_made, 1)
                pool.wait_ge(var_eps_made, s + 1)
                pool.tensor_tensor(rstd[:, :], var_eps[:, :], minus_half[:, :], ALU.pow).then_inc(rstd_made, 1)

            pool.wait_ge(ids_made, 2)
            rest_of_x(0, 0, 0)
            fold_w0(0, 0)
            fold_w2(0, 0, 0)
            rest_of_x(1, 1, 1)
            fold_w0(1, 1)
            fold_w2(1, 1, 1)
            pool.tensor_tensor(power[:, LATER:], amp_col.broadcast_to([N, B - LATER]), dt_sb[:, LATER:], ALU.pow)\
                .then_inc(power_made, 1)
            pool.wait_ge(bup_loaded, 16)

            def step(s, k, j):
                def x_and_w2():
                    rest_of_x(s + 2, k + 2, j + 2)
                    fold_w2(s + 2, k + 2, j + 2)

                if k < LAST - 1:
                    fold_w0(s + 2, k + 2)
                if k < 2:
                    x_and_w2()
                lang = language_of(pool, s)
                if k >= YB:
                    pool.wait_ge(out_stored[j % YB], loads_of(j, s, YB) - 16)
                pool.wait_ge(x3_made, s + 1)
                pool.tensor_tensor(yb[j % YB][:, :], x3[j % YB][:, :], bup_sb[:, bass.ds(lang * D, D)], ALU.add)\
                    .then_inc(x3bias_made, 1)
                if k == 0:
                    pool.wait_ge(beta_loaded, 16)
                pool.wait_ge(x3T_done, s + 1)
                pool.wait_ge(x3bias_made, s + 1)
                pool.tensor_tensor(x3[j % YB][:, :], x3[j % YB][:, :], beta_sb[:, bass.ds(lang * D, D)], ALU.add)\
                    .then_inc(x3beta_made, 1)
                if 2 <= k < LAST - 1:
                    x_and_w2()
                if k >= 1:
                    inverse_deviation(s - 1)

            over_samples(step)(pool)
            inverse_deviation(LAST)

        @block.scalar
        def _(act):
            act.wait_ge(angles_reduced, 1)
            act.activation(sine, angle_sin, ACT.Sin).then_inc(trig_made, 1)
            act.wait_ge(angles_reduced, 2)
            act.activation(cosine, angle_cos, ACT.Sin).then_inc(trig_made, 1)
            act.wait_ge(coef_made, 2)
            act.wait_ge(consts_made, 3)

            def make_diag(s, k):
                if k >= 1:
                    act.wait_ge(mix_made, s)
                act.activation(diag[:, :], ident[:, :], ACT.Copy, scale=cos1[:, bass.ds(s, 1)])\
                    .then_inc(diag_made, 1)

            def round_x(s, k, j):
                act.wait_ge(x_loaded[j % XB], loads_of(j, s, XB))
                if k >= 1:
                    act.wait_ge(l0_done, s)
                act.activation(x_hi[:, :], x_in[j % XB][:, :], ACT.Copy).then_inc(x_hi_made, 1)

            def round_w0(s, k):
                act.wait_ge(w0_folded, s + 1)
                if k == 0:
                    for half in halves:
                        act.activation(w0_hi[:, half], w0_in[:, half], ACT.Copy).then_inc(w0_hi_made, 1)
                    return
                act.wait_ge(l0_done, s)
                first = is_first(act, s)
                with act.If(first):
                    for half in halves:
                        act.activation(w0_hi[:, half], w0_in[:, half], ACT.Copy).then_inc(w0_hi_made, 1)
                with act.Else():
                    act.sem_inc(w0_hi_made, 2)

            def round_w2(s, k, j, n):
                if n == 0:
                    act.wait_ge(w2_folded, s + 1)
                    if k >= 1:
                        act.wait_ge(l2_done, s)
                act.activation(w2_hi[:, halves[n]], w2_in[j % 2][:, halves[n]], ACT.Copy).then_inc(w2_hi_made, 1)

            def round_x2T(s, k):
                act.wait_ge(mix_done, s + 1)
                if k >= 1:
                    act.wait_ge(l2_done, s)
                act.activation(x2T_hi[:, :], ps_mix[:, :], ACT.Copy).then_inc(x2T_hi_made, 1)

            round_x(0, 0, 0)
            round_w0(0, 0)
            make_diag(0, 0)
            round_w2(0, 0, 0, 0)
            round_w2(0, 0, 0, 1)
            round_x(1, 1, 1)
            round_x2T(0, 0)
            round_w0(1, 1)
            make_diag(1, 1)
            act.wait_ge(wup_loaded, 32)

            def step(s, k, j):
                if k == U - 1:
                    act.wait_ge(coef_made, 4)
                if k < LAST:
                    round_w2(s + 1, k + 1, j + 1, 0)
                act.wait_ge(x3T_done, s + 1)
                if k >= 1:
                    act.wait_ge(h_done, s)
                act.activation(x3T[:, :], ps_x3T[:, :], ACT.Copy).then_inc(x3T_made, 1)
                if k < LAST:
                    round_w2(s + 1, k + 1, j + 1, 1)
                if k < LAST - 1:
                    round_x(s + 2, k + 2, j + 2)
                act.wait_ge(h_done, s + 1)
                if k >= 1:
                    act.wait_ge(hT_done, s)
                act.activation(h[:, :], ps_h[:, :], ACT.Copy).then_inc(h_made, 1)
                if k < LAST:
                    round_x2T(s + 1, k + 1)
                lang = language_of(act, s)
                act.wait_ge(hT_done, s + 1)
                if k >= 1:
                    act.wait_ge(up_done, s)
                act.activation(hT[:, :], ps_hT[:, :], ACT.Relu, bias=b1_sb[:, bass.ds(lang, 1)]).then_inc(hT_made, 1)
                if k < LAST - 1:
                    make_diag(s + 2, k + 2)
                    round_w0(s + 2, k + 2)

            over_samples(step)(act)

        @block.vector
        def _(dve):
            chain = [0]

            def link(ins):
                chain[0] += 1
                ins.then_inc(chained, 1)
                dve.wait_ge(chained, chain[0])

            dve.wait_ge(small_loaded, 16 * 7)
            dve.wait_ge(places_made, 2)
            link(dve.tensor_copy(cols[:, 0:4], icols[:, :]))
            link(dve.tensor_copy(place_row, irows[:, 0:B]))
            link(dve.tensor_copy(subject_row, irows[:, B:2 * B]))
            link(dve.scalar_tensor_tensor(out=key_row, in0=subject_row, scalar=float(B), in1=place_row,
                                          op0=ALU.mult, op1=ALU.add))
            link(dve.scalar_tensor_tensor(out=key_col, in0=cols[:, 1:2], scalar=float(B), in1=cols[:, 0:1],
                                          op0=ALU.mult, op1=ALU.add))
            link(dve.tensor_scalar(compared, key_row, key_col, None, ALU.is_lt))
            link(dve.tensor_reduce(rank, compared, mybir.AxisListType.X, ALU.add))
            dve.tensor_scalar(onehot, place_row, rank, None, ALU.is_equal).then_inc(onehot_made, 1)
            dve.tensor_copy(dt_wide, dt_col.broadcast_to([P, P])).then_inc(onehot_made, 1)
            link(dve.tensor_scalar(compared, place_row, cols[:, 0:1], None, ALU.is_lt))
            link(dve.tensor_scalar(same, subject_row, cols[:, 1:2], None, ALU.is_equal))
            link(dve.tensor_tensor(same, same, compared, ALU.mult))
            link(dve.tensor_reduce(rank, same, mybir.AxisListType.X, ALU.add))
            dve.tensor_scalar(cols[:, 4:5], rank, 0.0, None, ALU.is_equal).then_inc(onehot_made, 1)
            dve.wait_ge(sorted_done, 1)
            dve.tensor_copy(ids[:, 0:4 * B], ps_l0[0:1, :]).then_inc(ids_made, 1)
            dve.tensor_copy(ids[:, 4 * B:5 * B], ps_l2[0:1, 0:B]).then_inc(ids_made, 1)
            dve.tensor_copy(dt_sb, ps_mix[:, 0:B]).then_inc(dt_made, 1)

            dve.wait_ge(dt_made, 1)
            link(dve.tensor_scalar(ang, dt_sb, freq_col, None, ALU.mult))
            for red, shift in ((angle_sin, 0.0), (angle_cos, 0.25)):
                link(dve.tensor_scalar(turns, ang, 0.5 / PI, shift, ALU.mult, ALU.add))
                link(dve.tensor_scalar(turns, turns, ROUND, None, ALU.add))
                link(dve.tensor_scalar(turns, turns, ROUND, None, ALU.subtract))
                link(dve.scalar_tensor_tensor(out=red, in0=turns, scalar=-TWO_PI[0], in1=ang,
                                              op0=ALU.mult, op1=ALU.add))
                for part in TWO_PI[1:]:
                    link(dve.scalar_tensor_tensor(out=red, in0=turns, scalar=-part, in1=red,
                                                  op0=ALU.mult, op1=ALU.add))
                link(dve.tensor_scalar(red, red, shift * 2 * PI, None, ALU.add))
                dve.tensor_scalar(red, red, PI_BELOW, -PI_BELOW, ALU.min, ALU.max).then_inc(angles_reduced, 1)

            def coefficients(places):
                dve.tensor_tensor(sin1[:, places], power[:, places], sine[:, places], ALU.mult).then_inc(coef_made, 1)
                link(dve.tensor_tensor(cosine[:, places], power[:, places], cosine[:, places], ALU.mult))
                dve.tensor_scalar(cos1[:, places], cosine[:, places], 1.0, None, ALU.add).then_inc(coef_made, 1)

            dve.wait_ge(power_made, 1)
            dve.wait_ge(trig_made, 2)
            coefficients(slice(0, SOON))
            dve.wait_ge(coef_made, 2)
            dve.wait_ge(consts_made, 3)

            def make_mix(s, k):
                dve.wait_ge(diag_made, s + 1)
                if k >= 1:
                    dve.wait_ge(mix_done, s)
                dve.scalar_tensor_tensor(out=mix[:, :], in0=signed_swap[:, :], scalar=sin1[:, bass.ds(s, 1)],
                                         in1=diag[:, :], op0=ALU.mult, op1=ALU.add).then_inc(mix_made, 1)

            def split_w0():
                for half in halves:
                    dve.tensor_tensor(w0_lo[:, half], w0_in[:, half], w0_hi[:, half].bitcast(fp32),
                                      ALU.subtract).then_inc(w0_lo_made, 1)
                dve.tensor_copy(b0_sb[:, :], b0_in[:, :]).then_inc(b0_made, 1)

            def rest_of_w0(s, k):
                dve.wait_ge(w0_hi_made, 2 * s + 2)
                if k == 0:
                    split_w0()
                    return
                dve.wait_ge(l0_done, s)
                dve.wait_ge(x1_made, s)
                first = is_first(dve, s)
                with dve.If(first):
                    split_w0()
                with dve.Else():
                    dve.sem_inc(w0_lo_made, 2)
                    dve.sem_inc(b0_made, 1)

            def rest_of_w2(s, j, n):
                half = halves[n]
                dve.wait_ge(w2_hi_made, 2 * s + n + 1)
                dve.tensor_tensor(w2_lo[:, half], w2_in[j % 2][:, half], w2_hi[:, half].bitcast(fp32),
                                  ALU.subtract).then_inc(w2_lo_made, 1)

            def finish_l0(s, k):
                dve.wait_ge(b0_made, s + 1)
                dve.wait_ge(l0_done, s + 1)
                if k >= 1:
                    dve.wait_ge(mix_done, s)
                dve.tensor_tensor(x1[:, :], ps_l0[:, :], b0_sb[:, :], ALU.add).then_inc(x1_made, 1)

            def rest_of_x2T(s, k):
                dve.wait_ge(x2T_hi_made, s + 1)
                if k >= 1:
                    dve.wait_ge(l2_done, s)
                dve.tensor_tensor(x2T_lo[:, :], ps_mix[:, :], x2T_hi[:, :].bitcast(fp32), ALU.subtract)\
                    .then_inc(x2T_lo_made, 1)

            def finish_l2(s, k, j):
                dve.wait_ge(b2_loaded[j % 2], loads_of(j, s, 2))
                dve.wait_ge(l2_done, s + 1)
                dve.tensor_tensor(x3[j % YB][:, :], ps_l2[:, :], b2_in[j % 2][:, :], ALU.add).then_inc(x3_made, 1)

            def statistics(s, j):
                y = yb[j % YB]
                dve.wait_ge(up_done, s + 1)
                dve.wait_ge(x3bias_made, s + 1)
                dve.tensor_tensor(y[:, :], ps_up[:, :], y[:, :], ALU.add).then_inc(y_made, 1)
                dve.wait_ge(y_made, s + 1)
                dve.bn_stats(stats[:, :], y[:, :]).then_inc(stats_made, 1)

            def mean_and_variance(s):
                dve.wait_ge(coef_made, 2)
                dve.wait_ge(stats_made, s + 1)
                dve.bn_aggr(mean_var[:, :], stats[:, :]).then_inc(mean_made, 1)

            def centre(s, j):
                lang = language_of(dve, s)
                y = yb[j % YB]
                dve.wait_ge(mean_made, s + 1)
                dve.scalar_tensor_tensor(out=y[:, :], in0=y[:, :], scalar=mean_var[:, 0:1],
                                         in1=gamma_sb[:, bass.ds(lang * D, D)],
                                         op0=ALU.subtract, op1=ALU.mult).then_inc(scaled_made, 1)

            def finish_norm(s, j):
                y = yb[j % YB]
                dve.wait_ge(rstd_made, s + 1)
                dve.wait_ge(scaled_made, s + 1)
                dve.wait_ge(x3beta_made, s + 1)
                dve.scalar_tensor_tensor(out=y[:, :], in0=y[:, :], scalar=rstd[:, 0:1], in1=x3[j % YB][:, :],
                                         op0=ALU.mult, op1=ALU.add).then_inc(out_made, 1)

            rest_of_w0(0, 0)
            make_mix(0, 0)
            finish_l0(0, 0)
            rest_of_w2(0, 0, 0)
            rest_of_w2(0, 0, 1)
            rest_of_x2T(0, 0)
            rest_of_w0(1, 1)

            def step(s, k, j):
                if k == U - 1:
                    dve.wait_ge(power_made, 3)
                    coefficients(slice(SOON, B))
                    dve.wait_ge(coef_made, 4)
                finish_l2(s, k, j)
                if k == 2:
                    dve.wait_ge(gamma_loaded, 16)
                if k >= 2:
                    centre(s - 2, j - 2)
                if k < LAST:
                    make_mix(s + 1, k + 1)
                    rest_of_w2(s + 1, j + 1, 0)
                    finish_l0(s + 1, k + 1)
                    rest_of_w2(s + 1, j + 1, 1)
                if k >= 2:
                    finish_norm(s - 2, j - 2)
                if k < LAST:
                    rest_of_x2T(s + 1, k + 1)
                if k >= 1:
                    statistics(s - 1, j - 1)
                if k < LAST - 1:
                    rest_of_w0(s + 2, k + 2)
                if k >= 1:
                    mean_and_variance(s - 1)

            over_samples(step)(dve)
            centre(LAST - 1, LAST - 1)
            finish_norm(LAST - 1, LAST - 1)
            statistics(LAST, LAST)
            mean_and_variance(LAST)
            centre(LAST, LAST)
            finish_norm(LAST, LAST)

        @block.tensor
        def _(pe):
            pe.wait_ge(onehot_made, 3)
            for n in range(4):
                pe.matmul(ps_l0[0:1, n * B:(n + 1) * B], cols[:, n:n + 1], onehot, start=True, stop=True)
            pe.matmul(ps_l2[0:1, 0:B], cols[:, 4:5], onehot, start=True, stop=True)
            pe.matmul(ps_mix[:, 0:B], dt_wide, onehot, start=True, stop=True).then_inc(sorted_done, 1)
            pe.wait_ge(ids_made, 2)

            def l0(s, k, part):
                passes = [(x, w, c) for x, w in ((x_hi, w0_hi), (x_hi, w0_lo), (x_lo, w0_hi)) for c in range(C)]
                for n in range(part * 3 * C // 2, (part + 1) * 3 * C // 2):
                    x, w, c = passes[n]
                    if n == 0:
                        pe.wait_ge(x_hi_made, s + 1)
                        pe.wait_ge(w0_hi_made, 2 * s + 2)
                        if k >= 1:
                            pe.wait_ge(x1_made, s)
                    if n == C:
                        pe.wait_ge(w0_lo_made, 2 * s + 2)
                    if n == 2 * C:
                        pe.wait_ge(x_lo_made, s + 1)
                    mm = pe.matmul(ps_l0[:, :], x[:, c * N:(c + 1) * N], w[:, c * D:(c + 1) * D],
                                   start=(n == 0), stop=(n == 3 * C - 1))
                if part == 1:
                    mm.then_inc(l0_done, 1)

            def rotate(s, k):
                pe.wait_ge(x1_made, s + 1)
                pe.wait_ge(mix_made, s + 1)
                if k >= 1:
                    pe.wait_ge(x2T_lo_made, s)
                for c in range(C):
                    mm = pe.matmul(ps_mix[:, c * N:(c + 1) * N], x1[:, c * P:(c + 1) * P], mix[:, :],
                                   start=True, stop=True)
                mm.then_inc(mix_done, 1)

            def l2(s, k):
                pe.wait_ge(x2T_hi_made, s + 1)
                if k >= 1:
                    pe.wait_ge(x3_made, s)
                for n, (x, w) in enumerate(((x2T_hi, w2_hi), (x2T_hi, w2_lo), (x2T_lo, w2_hi))):
                    if n == 0:
                        pe.wait_ge(w2_hi_made, 2 * s + 2)
                    if n == 1:
                        pe.wait_ge(w2_lo_made, 2 * s + 2)
                    if n == 2:
                        pe.wait_ge(x2T_lo_made, s + 1)
                    for c in range(C):
                        mm = pe.matmul(ps_l2[:, :], x[:, c * N:(c + 1) * N], w[:, c * D:(c + 1) * D],
                                       start=(n == 0 and c == 0), stop=(n == 2 and c == C - 1))
                mm.then_inc(l2_done, 1)

            def transpose_x3(s, k, j):
                pe.wait_ge(x3_made, s + 1)
                if k >= 1:
                    pe.wait_ge(x3T_made, s)
                for c in range(C):
                    mm = pe.transpose(ps_x3T[:, c * N:(c + 1) * N], x3[j % YB][:, c * P:(c + 1) * P], ident[:, :])
                mm.then_inc(x3T_done, 1)

            def down(s, k):
                lang = language_of(pe, s)
                pe.wait_ge(x3T_made, s + 1)
                if k >= 1:
                    pe.wait_ge(h_made, s)
                for c in range(C):
                    mm = pe.matmul(ps_h[:, :], x3T[:, c * N:(c + 1) * N],
                                   w1_sb[:, bass.ds(lang * (C * A) + c * A, A)], start=(c == 0), stop=(c == C - 1))
                mm.then_inc(h_done, 1)

            def transpose_h(s, k):
                pe.wait_ge(h_made, s + 1)
                if k >= 1:
                    pe.wait_ge(hT_made, s)
                pe.transpose(ps_hT[:, :], h[:, :], ident[:, :]).then_inc(hT_done, 1)

            def up(s, k):
                lang = language_of(pe, s)
                pe.wait_ge(hT_made, s + 1)
                if k >= 1:
                    pe.wait_ge(y_made, s)
                pe.matmul(ps_up[:, :], hT[:, :], wup_sb[:, bass.ds(lang * D, D)], start=True, stop=True)\
                    .then_inc(up_done, 1)

            pe.wait_ge(dt_made, 1)
            pe.wait_ge(consts_made, 3)
            l0(0, 0, 0)
            l0(0, 0, 1)
            rotate(0, 0)
            l2(0, 0)

            def step(s, k, j):
                if k < LAST:
                    l0(s + 1, k + 1, 0)
                transpose_x3(s, k, j)
                if k < LAST:
                    l0(s + 1, k + 1, 1)
                if k == 0:
                    pe.wait_ge(w1_loaded, 16)
                down(s, k)
                if k < LAST:
                    rotate(s + 1, k + 1)
                transpose_h(s, k)
                if k == 1:
                    pe.wait_ge(wup_loaded, 32)
                if k >= 1:
                    up(s - 1, k - 1)
                if k < LAST:
                    l2(s + 1, k + 1)

            over_samples(step)(pe)
            up(LAST, LAST)


def kernel(**inputs):
    import numpy as _np
    import concourse.bacc as _bacc
    from concourse import mybir as _mybir
    from concourse.bass_utils import run_bass_kernel_spmd as _run

    a = {name: _np.asarray(v) for name, v in inputs.items()}
    x = a["x"]
    B, N, D = x.shape
    P = 128
    C = D // P

    def feature_major(w):
        n, _, cols = w.shape
        return w.reshape(n, C, P, cols).transpose(0, 2, 1, 3)

    arrays = {
        "xT": feature_major(x.transpose(0, 2, 1)),
        "subject": a["itok_B_0_7"].reshape(1, B),
        "category": a["itok_B_0_63"].reshape(1, B),
        "language": a["itok_B_0_8"].reshape(1, B),
        "delta_t": a["condB_deltat"].reshape(1, B),
        "W0T": feature_major(a["L0_cond_weight"].transpose(0, 2, 1)),
        "b0": a["L0_cond_bias"],
        "amp_tok": _np.repeat(a["L1_cond_amplitudes"], 2).reshape(N, 1),
        "freq_tok": _np.repeat(a["L1_cond_frequencies"], 2).reshape(N, 1),
        "W2": feature_major(a["L2_cond_W"]),
        "b2": a["L2_cond_b"],
        "W1": feature_major(a["L3_cond_W1"]).transpose(1, 0, 2, 3),
        "b1T": a["L3_cond_b1"].transpose(1, 0),
        "Wup": a["L3_cond_W2"].transpose(1, 0, 2),
        "bup": a["L3_cond_b2"],
        "gamma": a["L3_cond_gamma"],
        "beta": a["L3_cond_beta"],
    }
    nc = _bacc.Bacc("TRN2", target_bir_lowering=False, num_devices=1,
                     dynamic_dma_scratch_size=1024)
    args = []
    for name in arrays:
        arrays[name] = _np.ascontiguousarray(arrays[name])
        args.append(nc.dram_tensor(name, arrays[name].shape, _mybir.dt.from_np(arrays[name].dtype),
                                   kind="ExternalInput").ap())
    args.append(nc.dram_tensor("out", (B, N, D), fp32, kind="ExternalOutput").ap())
    conditioned_residual_stack(nc, *args)
    r = _run(nc, [arrays], core_ids=[0])
    return r.results[0]["out"]
```

```python
import concourse.bass as bass
from concourse import mybir
from contextlib import ExitStack

fp32 = mybir.dt.float32
fp32r = mybir.dt.float32r
i32 = mybir.dt.int32
ALU = mybir.AluOpType
ACT = mybir.ActivationFunctionType

LN_EPS = 1e-5
PI = 3.14159265358979
PI_BELOW = 3.1415925
TWO_PI = (6.28125, 1.9350051879882812e-3, 3.0199159819388e-7)
ROUND = 12582912.0


def conditioned_residual_stack(
    nc: bass.Bass,
    xT: bass.AP,
    subject: bass.AP,
    category: bass.AP,
    language: bass.AP,
    delta_t: bass.AP,
    W0T: bass.AP,
    b0: bass.AP,
    amp_tok: bass.AP,
    freq_tok: bass.AP,
    W2: bass.AP,
    b2: bass.AP,
    W1: bass.AP,
    b1T: bass.AP,
    Wup: bass.AP,
    bup: bass.AP,
    gamma: bass.AP,
    beta: bass.AP,
    out: bass.AP,
):
    B, P, C, N = xT.shape
    S, D = b0.shape
    K = b2.shape[0]
    L, A = b1T.shape[1], b1T.shape[0]
    U = 8
    YB = 4
    SOON, LATER = 2 * YB, B // 4
    XB = 4
    LAST = B - 1
    WD = C * D

    ctx = ExitStack()
    with ctx:
        def sb(name, shape, dt=fp32):
            return ctx.enter_context(nc.sbuf_tensor(name, shape, dt))

        def pb(name, shape):
            return ctx.enter_context(nc.psum_tensor(name, shape, fp32))

        def sem(name):
            return ctx.enter_context(nc.semaphore(name))

        w1_sb = sb("w1_sb", [P, L * C * A])
        wup_sb = sb("wup_sb", [A, L * D])
        bup_sb = sb("bup_sb", [P, L * D])
        gamma_sb = sb("gamma_sb", [P, L * D])
        beta_sb = sb("beta_sb", [P, L * D])
        b1_sb = sb("b1_sb", [A, L])
        ident = sb("ident", [P, P])
        signed_swap = sb("signed_swap", [N, N])
        ids = sb("ids", [1, 6 * B], i32)
        cos1 = sb("cos1", [N, B])
        sin1 = sb("sin1", [N, B])
        eps = sb("eps", [N, 1])
        minus_half = sb("minus_half", [N, 1])
        w0_in = sb("w0_in", [P, WD])
        b0_in = sb("b0_in", [P, D])
        w0_hi = sb("w0_hi", [P, WD], fp32r)
        w0_lo = sb("w0_lo", [P, WD], fp32r)
        b0_sb = sb("b0_sb", [P, D])
        x_in = [sb(f"x_in{i}", [P, C * N]) for i in range(XB)]
        x_hi = sb("x_hi", [P, C * N], fp32r)
        x_lo = sb("x_lo", [P, C * N], fp32r)
        w2_in = [sb(f"w2_in{i}", [P, WD]) for i in range(2)]
        w2_hi = sb("w2_hi", [P, WD], fp32r)
        w2_lo = sb("w2_lo", [P, WD], fp32r)
        b2_in = [sb(f"b2_in{i}", [P, D]) for i in range(2)]
        x1 = sb("x1", [N, D])
        diag = sb("diag", [N, N])
        mix = sb("mix", [N, N])
        x2T_hi = sb("x2T_hi", [P, C * N], fp32r)
        x2T_lo = sb("x2T_lo", [P, C * N], fp32r)
        x3 = [sb(f"x3_{i}", [N, D]) for i in range(YB)]
        x3T = sb("x3T", [P, C * N])
        h = sb("h", [N, A])
        hT = sb("hT", [A, N])
        yb = [sb(f"yb{i}", [N, D]) for i in range(YB)]
        stats = sb("stats", [N, 6])
        mean_var = sb("mean_var", [N, 2])
        var_eps = sb("var_eps", [N, 1])
        rstd = sb("rstd", [N, 1])

        ps_l0 = pb("ps_l0", [N, D])
        ps_mix = pb("ps_mix", [P, C * N])
        ps_l2 = pb("ps_l2", [N, D])
        ps_x3T = pb("ps_x3T", [P, C * N])
        ps_h = pb("ps_h", [N, A])
        ps_hT = pb("ps_hT", [A, N])
        ps_up = pb("ps_up", [N, D])

        def column(n):
            return stats_cols[:, n:n + 1]

        stats_cols = sb("stats_cols", [P, 16])
        icols = stats_cols[:, 8:12].bitcast(i32)
        cols = stats_cols[:, 0:5]
        dt_col, amp_col, freq_col = (stats_cols[:, n:n + 1] for n in (5, 6, 7))
        key_col, rank, earlier = (stats_cols[:, n:n + 1] for n in (12, 13, 14))
        irows = x3[0][:, 0:2 * B].bitcast(i32)
        place_row = x3[0][:, 2 * B:3 * B]
        subject_row = x3[0][:, 3 * B:4 * B]
        key_row = x3T[:, 0:B]
        compared = x3T[:, B:2 * B]
        same = x3T[:, 2 * B:3 * B]
        dt_wide = x3T[:, 3 * B:4 * B]
        onehot = h[:, :]
        reached = mix[:, :]
        ang, turns, angle_sin, angle_cos = (x1[:, n * B:(n + 1) * B] for n in range(4))
        dt_sb, power, sine, cosine = (x3[YB - 1][:, n * B:(n + 1) * B] for n in range(4))

        small_loaded = sem("small_loaded")
        w1_loaded = sem("w1_loaded")
        bup_loaded = sem("bup_loaded")
        wup_loaded = sem("wup_loaded")
        b1_loaded = sem("b1_loaded")
        beta_loaded = sem("beta_loaded")
        gamma_loaded = sem("gamma_loaded")
        w0_loaded = sem("w0_loaded")
        x_loaded = [sem(f"x_loaded{i}") for i in range(XB)]
        w2_loaded = [sem(f"w2_loaded{i}") for i in range(2)]
        b2_loaded = [sem(f"b2_loaded{i}") for i in range(2)]
        out_stored = [sem(f"out_stored{i}") for i in range(YB)]
        zeroed = sem("zeroed")
        consts_made = sem("consts_made")
        places_made = sem("places_made")
        onehot_made = sem("onehot_made")
        sorted_done = sem("sorted_done")
        ids_made = sem("ids_made")
        dt_made = sem("dt_made")
        power_made = sem("power_made")
        chained = sem("chained")
        angles_reduced = sem("angles_reduced")
        trig_made = sem("trig_made")
        coef_made = sem("coef_made")
        w0_folded = sem("w0_folded")
        w0_hi_made = [sem(f"w0_hi_made{half}") for half in range(2)]
        w0_lo_made = sem("w0_lo_made")
        b0_made = sem("b0_made")
        x_hi_made = sem("x_hi_made")
        x_lo_made = sem("x_lo_made")
        l0_done = sem("l0_done")
        mix_done = sem("mix_done")
        l2_done = sem("l2_done")
        x3T_done = sem("x3T_done")
        h_done = sem("h_done")
        hT_done = sem("hT_done")
        up_done = sem("up_done")
        x1_made = sem("x1_made")
        diag_made = sem("diag_made")
        mix_made = sem("mix_made")
        x2T_hi_made = sem("x2T_hi_made")
        x2T_lo_made = sem("x2T_lo_made")
        w2_folded = sem("w2_folded")
        w2_hi_made = sem("w2_hi_made")
        w2_lo_made = sem("w2_lo_made")
        x3_made = sem("x3_made")
        x3T_made = sem("x3T_made")
        h_made = sem("h_made")
        hT_made = sem("hT_made")
        x3bias_made = sem("x3bias_made")
        x3beta_made = sem("x3beta_made")
        y_made = sem("y_made")
        stats_made = sem("stats_made")
        mean_made = sem("mean_made")
        var_eps_made = sem("var_eps_made")
        rstd_made = sem("rstd_made")
        scaled_made = sem("scaled_made")
        out_made = sem("out_made")

        block = ctx.enter_context(nc.Block())

        def sample_of(eng, s):
            return eng.value_load(ids[0:1, bass.ds(s, 1)], min_val=0, max_val=B - 1)

        def subject_of(eng, s):
            return eng.value_load(ids[0:1, bass.ds(B + s, 1)], min_val=0, max_val=S - 1)

        def category_of(eng, s):
            return eng.value_load(ids[0:1, bass.ds(2 * B + s, 1)], min_val=0, max_val=K - 1)

        def language_of(eng, s):
            return eng.value_load(ids[0:1, bass.ds(3 * B + s, 1)], min_val=0, max_val=L - 1)

        def is_first(eng, s):
            return eng.value_load(ids[0:1, bass.ds(4 * B + s, 1)], min_val=0, max_val=1)

        def ordinal_of(eng, s):
            return eng.value_load(ids[0:1, bass.ds(5 * B + s, 1)], min_val=1, max_val=S)

        def diagonal_of(tile):
            return bass.AP(tile[:, :].tensor, 0, [[WD, P], [D + P, C], [1, P]])

        def loads_of(j, s, n):
            return (s - j) * (16 // n) + 16 * (j // n) + 16

        halves = (slice(0, WD // 2), slice(WD // 2, WD))
        row_halves = (slice(0, D // 2), slice(D // 2, D))

        def over_samples(step):
            def run(eng):
                for s in range(U):
                    step(s, s, s)
                with nc.Fori(U, B - 2 * U + 1, U, engines=[eng.engine]) as i:
                    for j in range(U):
                        step(i + j, U, j)
                for j in range(U):
                    step(B - U + j, B - U + j, j)
            return run

        @block.sync
        def _(sp):
            sp.dma_start(irows[:, B:2 * B], subject.partition_broadcast(P)).then_inc(small_loaded, 16)
            for n, ids_dram in enumerate((subject, category, language)):
                sp.dma_start(icols[:, n + 1:n + 2], ids_dram.rearrange("a b -> b a")).then_inc(small_loaded, 16)
            sp.dma_start(dt_col, delta_t.rearrange("a b -> b a")).then_inc(small_loaded, 16)
            sp.dma_start(amp_col, amp_tok).then_inc(small_loaded, 16)
            sp.dma_start(freq_col, freq_tok).then_inc(small_loaded, 16)
            sp.dma_start(b1_sb[:, :], b1T).then_inc(b1_loaded, 16)
            sp.dma_start(w1_sb[:, :], W1.rearrange("p l c a -> p (l c a)")).then_inc(w1_loaded, 16)
            sp.dma_start(bup_sb[:, :], bup.rearrange("l d -> (l d)").partition_broadcast(P)).then_inc(bup_loaded, 16)
            sp.sem_inc(w0_lo_made, 2)
            sp.sem_inc(b0_made, 1)
            sp.wait_ge(ids_made, 2)

            def fetch_w0(sub):
                sp.dma_start(w0_in[:, :], W0T[bass.ds(sub, 1)].rearrange("o p c d -> p (o c d)")).then_inc(w0_loaded, 16)
                sp.dma_start(b0_in[:, :], b0[bass.ds(sub, 1)].rearrange("o d -> (o d)").partition_broadcast(P))\
                    .then_inc(w0_loaded, 16)

            def subject_words(s):
                return is_first(sp, s), subject_of(sp, s), ordinal_of(sp, s)

            def load_w0(words):
                first, sub, ordinal = words
                with sp.If(first):
                    sp.wait_ge(w0_lo_made, 2 * ordinal)
                    sp.wait_ge(b0_made, ordinal)
                    fetch_w0(sub)

            def load_x(s, k, j):
                if k >= XB:
                    sp.wait_ge(x_lo_made, s - XB + 1)
                sp.dma_start(x_in[j % XB][:, :], xT[bass.ds(sample_of(sp, s), 1)].rearrange("o p c n -> p (o c n)"))\
                    .then_inc(x_loaded[j % XB], 16)

            def load_w2(s, k, j):
                cat = category_of(sp, s)
                if k >= 2:
                    sp.wait_ge(w2_lo_made, 2 * s - 2)
                sp.dma_start(w2_in[j % 2][:, :], W2[bass.ds(cat, 1)].rearrange("o p c d -> p (o c d)"))\
                    .then_inc(w2_loaded[j % 2], 16)

            def load_b2(s, k, j):
                cat = category_of(sp, s)
                if k >= 2:
                    sp.wait_ge(x3_made, s - 1)
                sp.dma_start(b2_in[j % 2][:, :], b2[bass.ds(cat, 1)].rearrange("o d -> (o d)").partition_broadcast(P))\
                    .then_inc(b2_loaded[j % 2], 16)

            def store_out(s, j):
                sample = sample_of(sp, s)
                sp.wait_ge(out_made, s + 1)
                sp.dma_start(out[bass.ds(sample, 1)].rearrange("o n d -> n (o d)"), yb[j % YB][:, :])\
                    .then_inc(out_stored[j % YB], 16)

            load_x(0, 0, 0)
            fetch_w0(subject_of(sp, 0))
            load_w2(0, 0, 0)
            load_b2(0, 0, 0)
            load_x(1, 1, 1)
            load_w2(1, 1, 1)
            load_b2(1, 1, 1)
            load_x(2, 2, 2)
            load_w0(subject_words(1))
            sp.dma_start(beta_sb[:, :], beta.rearrange("l d -> (l d)").partition_broadcast(P)).then_inc(beta_loaded, 16)
            sp.dma_start(wup_sb[:, :], Wup.rearrange("p l d -> p (l d)")).then_inc(wup_loaded, 16)
            load_x(3, 3, 3)
            load_w0(subject_words(2))
            load_w0(subject_words(3))

            def step(s, k, j):
                if k < LAST - 3:
                    words = subject_words(s + 4)
                if k < LAST - 1:
                    load_w2(s + 2, k + 2, j + 2)
                if k >= 2:
                    store_out(s - 2, j - 2)
                if k < LAST - 1:
                    load_b2(s + 2, k + 2, j + 2)
                if k == 0:
                    sp.dma_start(gamma_sb[:, :], gamma.rearrange("l d -> (l d)").partition_broadcast(P))\
                        .then_inc(gamma_loaded, 16)
                if k < LAST - 3:
                    load_x(s + 4, k + 4, j + 4)
                if k < LAST - 3:
                    load_w0(words)

            over_samples(step)(sp)
            for s in range(B - 2, B):
                store_out(s, s)
            for b in range(YB):
                sp.wait_ge(out_stored[b], 16 * (B // YB))

        @block.gpsimd
        def _(pool):
            pool.iota(icols[:, 0:1], pattern=[[0, 1]], base=0, channel_multiplier=1).then_inc(places_made, 1)
            pool.iota(irows[:, 0:B], pattern=[[1, B]], base=0, channel_multiplier=0).then_inc(places_made, 1)
            pool.memset(ident[:, :], 0.0).then_inc(zeroed, 1)
            pool.memset(signed_swap[:, :], 0.0).then_inc(zeroed, 1)
            pool.memset(minus_half[:, :], -0.5).then_inc(zeroed, 1)
            pool.memset(eps[:, :], LN_EPS).then_inc(zeroed, 1)
            pool.wait_ge(zeroed, 4)
            pool.affine_select(out=ident[:, :], in_=ident[:, :], compare_op=ALU.not_equal, fill=1.0,
                               base=0, pattern=[[-1, P]], channel_multiplier=1).then_inc(consts_made, 1)
            pairs = signed_swap[:, :].rearrange("p (f e) -> p e f", e=2)
            pool.affine_select(out=pairs[:, 1], in_=pairs[:, 1], compare_op=ALU.not_equal, fill=1.0,
                               base=0, pattern=[[-2, N // 2]], channel_multiplier=1).then_inc(consts_made, 1)
            pool.affine_select(out=pairs[:, 0], in_=pairs[:, 0], compare_op=ALU.not_equal, fill=-1.0,
                               base=-1, pattern=[[-2, N // 2]], channel_multiplier=1).then_inc(consts_made, 1)
            pool.wait_ge(dt_made, 1)
            for places in (slice(0, SOON), slice(SOON, LATER)):
                pool.tensor_tensor(power[:, places], amp_col.broadcast_to([N, places.stop - places.start]),
                                   dt_sb[:, places], ALU.pow).then_inc(power_made, 1)
            pool.wait_ge(consts_made, 3)

            def fold_w0(s, k):
                if k == 0:
                    pool.wait_ge(w0_loaded, 32)
                    pool.tensor_tensor(diagonal_of(w0_in), diagonal_of(w0_in),
                                       ident[:, :].unsqueeze(1).broadcast_to([P, C, P]), ALU.add).then_inc(w0_folded, 1)
                    return
                first = is_first(pool, s)
                with pool.If(first):
                    ordinal = ordinal_of(pool, s)
                    pool.wait_ge(w0_loaded, 32 * ordinal)
                    pool.tensor_tensor(diagonal_of(w0_in), diagonal_of(w0_in),
                                       ident[:, :].unsqueeze(1).broadcast_to([P, C, P]), ALU.add).then_inc(w0_folded, 1)

            def fold_w2(s, k, j):
                pool.wait_ge(w2_loaded[j % 2], loads_of(j, s, 2))
                pool.tensor_tensor(diagonal_of(w2_in[j % 2]), diagonal_of(w2_in[j % 2]),
                                   ident[:, :].unsqueeze(1).broadcast_to([P, C, P]), ALU.add).then_inc(w2_folded, 1)

            def rest_of_x(s, k, j):
                pool.wait_ge(x_hi_made, s + 1)
                if k >= 1:
                    pool.wait_ge(l0_done, s)
                pool.tensor_tensor(x_lo[:, :], x_in[j % XB][:, :], x_hi[:, :].bitcast(fp32), ALU.subtract).then_inc(x_lo_made, 1)

            def inverse_deviation(s):
                pool.wait_ge(mean_made, s + 1)
                pool.tensor_tensor(var_eps[:, :], mean_var[:, 1:2], eps[:, :], ALU.add).then_inc(var_eps_made, 1)
                pool.wait_ge(var_eps_made, s + 1)
                pool.tensor_tensor(rstd[:, :], var_eps[:, :], minus_half[:, :], ALU.pow).then_inc(rstd_made, 1)

            pool.wait_ge(ids_made, 2)
            rest_of_x(0, 0, 0)
            fold_w0(0, 0)
            fold_w2(0, 0, 0)
            rest_of_x(1, 1, 1)
            fold_w0(1, 1)
            fold_w2(1, 1, 1)
            fold_w0(2, 2)
            pool.tensor_tensor(power[:, LATER:], amp_col.broadcast_to([N, B - LATER]), dt_sb[:, LATER:], ALU.pow)\
                .then_inc(power_made, 1)
            pool.wait_ge(bup_loaded, 16)

            def step(s, k, j):
                def x_and_w2():
                    rest_of_x(s + 2, k + 2, j + 2)
                    fold_w2(s + 2, k + 2, j + 2)

                if k < 2:
                    x_and_w2()
                lang = language_of(pool, s)
                if k >= YB:
                    pool.wait_ge(out_stored[j % YB], loads_of(j, s, YB) - 16)
                pool.wait_ge(x3_made, s + 1)
                pool.tensor_tensor(yb[j % YB][:, :], x3[j % YB][:, :], bup_sb[:, bass.ds(lang * D, D)], ALU.add)\
                    .then_inc(x3bias_made, 1)
                if k == 0:
                    pool.wait_ge(beta_loaded, 16)
                pool.wait_ge(x3T_done, s + 1)
                pool.wait_ge(x3bias_made, s + 1)
                pool.tensor_tensor(x3[j % YB][:, :], x3[j % YB][:, :], beta_sb[:, bass.ds(lang * D, D)], ALU.add)\
                    .then_inc(x3beta_made, 1)
                if 2 <= k < LAST - 1:
                    x_and_w2()
                if k >= 1:
                    inverse_deviation(s - 1)
                if k < LAST - 2:
                    fold_w0(s + 3, k + 3)

            over_samples(step)(pool)
            inverse_deviation(LAST)

        @block.scalar
        def _(act):
            act.wait_ge(angles_reduced, 1)
            act.activation(sine, angle_sin, ACT.Sin).then_inc(trig_made, 1)
            act.wait_ge(angles_reduced, 2)
            act.activation(cosine, angle_cos, ACT.Sin).then_inc(trig_made, 1)
            act.wait_ge(coef_made, 2)
            act.wait_ge(consts_made, 3)

            def make_diag(s, k):
                if k >= 1:
                    act.wait_ge(mix_made, s)
                act.activation(diag[:, :], ident[:, :], ACT.Copy, scale=cos1[:, bass.ds(s, 1)])\
                    .then_inc(diag_made, 1)

            def round_x(s, k, j):
                act.wait_ge(x_loaded[j % XB], loads_of(j, s, XB))
                if k >= 1:
                    act.wait_ge(l0_done, s)
                act.activation(x_hi[:, :], x_in[j % XB][:, :], ACT.Copy).then_inc(x_hi_made, 1)

            def convert_w0():
                for n, half in enumerate(halves):
                    act.activation(w0_hi[:, half], w0_in[:, half], ACT.Copy).then_inc(w0_hi_made[n], 1)
                act.activation(b0_sb[:, :], b0_in[:, :], ACT.Copy).then_inc(b0_made, 1)

            def round_w0(s, k):
                if k == 0:
                    act.wait_ge(w0_folded, 1)
                    convert_w0()
                    return
                first = is_first(act, s)
                with act.If(first):
                    ordinal = ordinal_of(act, s)
                    act.wait_ge(w0_folded, ordinal)
                    act.wait_ge(l0_done, s)
                    act.wait_ge(x1_made, 2 * s)
                    convert_w0()

            def round_w2(s, k, j, n):
                if n == 0:
                    act.wait_ge(w2_folded, s + 1)
                    if k >= 1:
                        act.wait_ge(l2_done, s)
                act.activation(w2_hi[:, halves[n]], w2_in[j % 2][:, halves[n]], ACT.Copy).then_inc(w2_hi_made, 1)

            def round_x2T(s, k):
                act.wait_ge(mix_done, s + 1)
                if k >= 1:
                    act.wait_ge(l2_done, s)
                for half in row_halves:
                    act.activation(x2T_hi[:, half], ps_mix[:, half], ACT.Copy).then_inc(x2T_hi_made, 1)

            round_x(0, 0, 0)
            round_w0(0, 0)
            make_diag(0, 0)
            round_w2(0, 0, 0, 0)
            round_w2(0, 0, 0, 1)
            round_x(1, 1, 1)
            round_x2T(0, 0)
            round_w0(1, 1)
            make_diag(1, 1)
            act.wait_ge(b1_loaded, 16)

            def step(s, k, j):
                if k == YB - 1:
                    act.wait_ge(coef_made, 4)
                if k < LAST:
                    round_w2(s + 1, k + 1, j + 1, 0)
                act.wait_ge(x3T_done, s + 1)
                if k >= 1:
                    act.wait_ge(h_done, s)
                act.activation(x3T[:, :], ps_x3T[:, :], ACT.Copy).then_inc(x3T_made, 1)
                if k < LAST:
                    round_w2(s + 1, k + 1, j + 1, 1)
                if k < LAST - 1:
                    round_x(s + 2, k + 2, j + 2)
                act.wait_ge(h_done, s + 1)
                if k >= 1:
                    act.wait_ge(hT_done, s)
                act.activation(h[:, :], ps_h[:, :], ACT.Copy).then_inc(h_made, 1)
                if k < LAST:
                    round_x2T(s + 1, k + 1)
                lang = language_of(act, s)
                act.wait_ge(hT_done, s + 1)
                if k >= 1:
                    act.wait_ge(up_done, s)
                act.activation(hT[:, :], ps_hT[:, :], ACT.Relu, bias=b1_sb[:, bass.ds(lang, 1)]).then_inc(hT_made, 1)
                if k < LAST - 1:
                    make_diag(s + 2, k + 2)
                    round_w0(s + 2, k + 2)

            over_samples(step)(act)

        @block.vector
        def _(dve):
            chain = [0]

            def link(ins):
                chain[0] += 1
                ins.then_inc(chained, 1)
                dve.wait_ge(chained, chain[0])

            dve.wait_ge(small_loaded, 16 * 7)
            dve.wait_ge(places_made, 2)
            link(dve.tensor_copy(cols[:, 0:4], icols[:, :]))
            link(dve.tensor_copy(place_row, irows[:, 0:B]))
            link(dve.tensor_copy(subject_row, irows[:, B:2 * B]))
            link(dve.scalar_tensor_tensor(out=key_row, in0=subject_row, scalar=float(B), in1=place_row,
                                          op0=ALU.mult, op1=ALU.add))
            link(dve.scalar_tensor_tensor(out=key_col, in0=cols[:, 1:2], scalar=float(B), in1=cols[:, 0:1],
                                          op0=ALU.mult, op1=ALU.add))
            link(dve.tensor_scalar(compared, key_row, key_col, None, ALU.is_lt))
            link(dve.tensor_reduce(rank, compared, mybir.AxisListType.X, ALU.add))
            dve.tensor_scalar(onehot, place_row, rank, None, ALU.is_equal).then_inc(onehot_made, 1)
            dve.tensor_copy(dt_wide, dt_col.broadcast_to([P, P])).then_inc(onehot_made, 1)
            dve.tensor_scalar(reached, place_row, rank, None, ALU.is_ge).then_inc(onehot_made, 1)
            link(dve.tensor_scalar(compared, place_row, cols[:, 0:1], None, ALU.is_lt))
            link(dve.tensor_scalar(same, subject_row, cols[:, 1:2], None, ALU.is_equal))
            link(dve.tensor_tensor(same, same, compared, ALU.mult))
            link(dve.tensor_reduce(earlier, same, mybir.AxisListType.X, ALU.add))
            dve.tensor_scalar(cols[:, 4:5], earlier, 0.0, None, ALU.is_equal).then_inc(onehot_made, 1)
            dve.wait_ge(sorted_done, 1)
            dve.tensor_copy(ids[:, 0:4 * B], ps_l0[0:1, :]).then_inc(ids_made, 1)
            dve.tensor_copy(ids[:, 4 * B:6 * B], ps_l2[0:1, 0:2 * B]).then_inc(ids_made, 1)
            dve.tensor_copy(dt_sb, ps_mix[:, 0:B]).then_inc(dt_made, 1)

            dve.wait_ge(dt_made, 1)
            link(dve.tensor_scalar(ang, dt_sb, freq_col, None, ALU.mult))
            for red, shift in ((angle_sin, 0.0), (angle_cos, 0.25)):
                link(dve.tensor_scalar(turns, ang, 0.5 / PI, shift, ALU.mult, ALU.add))
                link(dve.tensor_scalar(turns, turns, ROUND, None, ALU.add))
                link(dve.tensor_scalar(turns, turns, ROUND, None, ALU.subtract))
                link(dve.scalar_tensor_tensor(out=red, in0=turns, scalar=-TWO_PI[0], in1=ang,
                                              op0=ALU.mult, op1=ALU.add))
                for part in TWO_PI[1:]:
                    link(dve.scalar_tensor_tensor(out=red, in0=turns, scalar=-part, in1=red,
                                                  op0=ALU.mult, op1=ALU.add))
                link(dve.tensor_scalar(red, red, shift * 2 * PI, None, ALU.add))
                dve.tensor_scalar(red, red, PI_BELOW, -PI_BELOW, ALU.min, ALU.max).then_inc(angles_reduced, 1)

            def coefficients(places):
                dve.tensor_tensor(sin1[:, places], power[:, places], sine[:, places], ALU.mult).then_inc(coef_made, 1)
                link(dve.tensor_tensor(cosine[:, places], power[:, places], cosine[:, places], ALU.mult))
                dve.tensor_scalar(cos1[:, places], cosine[:, places], 1.0, None, ALU.add).then_inc(coef_made, 1)

            dve.wait_ge(power_made, 1)
            dve.wait_ge(trig_made, 2)
            coefficients(slice(0, SOON))
            dve.wait_ge(coef_made, 2)
            dve.wait_ge(consts_made, 3)

            def make_mix(s, k):
                dve.wait_ge(diag_made, s + 1)
                if k >= 1:
                    dve.wait_ge(mix_done, s)
                dve.scalar_tensor_tensor(out=mix[:, :], in0=signed_swap[:, :], scalar=sin1[:, bass.ds(s, 1)],
                                         in1=diag[:, :], op0=ALU.mult, op1=ALU.add).then_inc(mix_made, 1)

            def split_w0(ordinal):
                for n, half in enumerate(halves):
                    dve.wait_ge(w0_hi_made[n], ordinal)
                    dve.tensor_tensor(w0_lo[:, half], w0_in[:, half], w0_hi[:, half].bitcast(fp32),
                                      ALU.subtract).then_inc(w0_lo_made, 1)

            def rest_of_w0(s, k):
                if k == 0:
                    split_w0(1)
                    return
                first = is_first(dve, s)
                with dve.If(first):
                    ordinal = ordinal_of(dve, s)
                    dve.wait_ge(l0_done, s)
                    split_w0(ordinal)

            def rest_of_w2(s, j, n):
                half = halves[n]
                dve.wait_ge(w2_hi_made, 2 * s + n + 1)
                dve.tensor_tensor(w2_lo[:, half], w2_in[j % 2][:, half], w2_hi[:, half].bitcast(fp32),
                                  ALU.subtract).then_inc(w2_lo_made, 1)

            def finish_l0(s, k):
                dve.wait_ge(l0_done, s + 1)
                if k >= 1:
                    dve.wait_ge(mix_done, s)
                for half in row_halves:
                    dve.tensor_tensor(x1[:, half], ps_l0[:, half], b0_sb[:, half], ALU.add).then_inc(x1_made, 1)

            def rest_of_x2T(s, k):
                dve.wait_ge(x2T_hi_made, 2 * s + 2)
                if k >= 1:
                    dve.wait_ge(l2_done, s)
                dve.tensor_tensor(x2T_lo[:, :], ps_mix[:, :], x2T_hi[:, :].bitcast(fp32), ALU.subtract)\
                    .then_inc(x2T_lo_made, 1)

            def finish_l2(s, k, j):
                dve.wait_ge(b2_loaded[j % 2], loads_of(j, s, 2))
                dve.wait_ge(l2_done, s + 1)
                dve.tensor_tensor(x3[j % YB][:, :], ps_l2[:, :], b2_in[j % 2][:, :], ALU.add).then_inc(x3_made, 1)

            def statistics(s, j):
                y = yb[j % YB]
                dve.wait_ge(up_done, s + 1)
                dve.wait_ge(x3bias_made, s + 1)
                dve.tensor_tensor(y[:, :], ps_up[:, :], y[:, :], ALU.add).then_inc(y_made, 1)
                dve.wait_ge(y_made, s + 1)
                dve.bn_stats(stats[:, :], y[:, :]).then_inc(stats_made, 1)

            def mean_and_variance(s):
                dve.wait_ge(coef_made, 2)
                dve.wait_ge(stats_made, s + 1)
                dve.bn_aggr(mean_var[:, :], stats[:, :]).then_inc(mean_made, 1)

            def centre(s, j):
                lang = language_of(dve, s)
                y = yb[j % YB]
                dve.wait_ge(mean_made, s + 1)
                dve.scalar_tensor_tensor(out=y[:, :], in0=y[:, :], scalar=mean_var[:, 0:1],
                                         in1=gamma_sb[:, bass.ds(lang * D, D)],
                                         op0=ALU.subtract, op1=ALU.mult).then_inc(scaled_made, 1)

            def finish_norm(s, j):
                y = yb[j % YB]
                dve.wait_ge(rstd_made, s + 1)
                dve.wait_ge(scaled_made, s + 1)
                dve.wait_ge(x3beta_made, s + 1)
                dve.scalar_tensor_tensor(out=y[:, :], in0=y[:, :], scalar=rstd[:, 0:1], in1=x3[j % YB][:, :],
                                         op0=ALU.mult, op1=ALU.add).then_inc(out_made, 1)

            rest_of_w0(0, 0)
            make_mix(0, 0)
            finish_l0(0, 0)
            rest_of_w2(0, 0, 0)
            rest_of_w2(0, 0, 1)
            rest_of_x2T(0, 0)
            rest_of_w0(1, 1)

            def step(s, k, j):
                if k == 2:
                    dve.wait_ge(gamma_loaded, 16)
                if k >= 2:
                    centre(s - 2, j - 2)
                if k < LAST:
                    make_mix(s + 1, k + 1)
                    rest_of_w2(s + 1, j + 1, 0)
                    finish_l0(s + 1, k + 1)
                    rest_of_w2(s + 1, j + 1, 1)
                if k >= 2:
                    finish_norm(s - 2, j - 2)
                if k < LAST:
                    rest_of_x2T(s + 1, k + 1)
                if k >= 1:
                    statistics(s - 1, j - 1)
                if k < LAST - 1:
                    rest_of_w0(s + 2, k + 2)
                if k >= 1:
                    mean_and_variance(s - 1)
                if k == YB - 2:
                    dve.wait_ge(power_made, 3)
                    coefficients(slice(SOON, B))
                    dve.wait_ge(coef_made, 4)
                if k < LAST:
                    finish_l2(s + 1, k + 1, j + 1)

            finish_l2(0, 0, 0)
            over_samples(step)(dve)
            centre(LAST - 1, LAST - 1)
            finish_norm(LAST - 1, LAST - 1)
            statistics(LAST, LAST)
            mean_and_variance(LAST)
            centre(LAST, LAST)
            finish_norm(LAST, LAST)

        @block.tensor
        def _(pe):
            pe.wait_ge(onehot_made, 4)
            for n in range(4):
                pe.matmul(ps_l0[0:1, n * B:(n + 1) * B], cols[:, n:n + 1], onehot, start=True, stop=True)
            pe.matmul(ps_l2[0:1, 0:B], cols[:, 4:5], onehot, start=True, stop=True)
            pe.matmul(ps_l2[0:1, B:2 * B], cols[:, 4:5], reached, start=True, stop=True)
            pe.matmul(ps_mix[:, 0:B], dt_wide, onehot, start=True, stop=True).then_inc(sorted_done, 1)
            pe.wait_ge(ids_made, 2)

            def l0(s, k, part, ordinal):
                passes = [(x, w, c) for x, w in ((x_hi, w0_hi), (x_hi, w0_lo), (x_lo, w0_hi)) for c in range(C)]
                for n in range(part * 3 * C // 2, (part + 1) * 3 * C // 2):
                    x, w, c = passes[n]
                    if n == 0:
                        pe.wait_ge(x_hi_made, s + 1)
                        pe.wait_ge(w0_hi_made[0], ordinal)
                        pe.wait_ge(w0_hi_made[1], ordinal)
                        if k >= 1:
                            pe.wait_ge(x1_made, 2 * s)
                    if n == C:
                        pe.wait_ge(w0_lo_made, 2 * ordinal + 2)
                    if n == 2 * C:
                        pe.wait_ge(b0_made, ordinal + 1)
                        pe.wait_ge(x_lo_made, s + 1)
                    mm = pe.matmul(ps_l0[:, :], x[:, c * N:(c + 1) * N], w[:, c * D:(c + 1) * D],
                                   start=(n == 0), stop=(n == 3 * C - 1))
                if part == 1:
                    mm.then_inc(l0_done, 1)

            def rotate(s, k):
                pe.wait_ge(mix_made, s + 1)
                if k >= 1:
                    pe.wait_ge(x2T_lo_made, s)
                for c in range(C):
                    if c in (0, C // 2):
                        pe.wait_ge(x1_made, 2 * s + 1 + c // (C // 2))
                    mm = pe.matmul(ps_mix[:, c * N:(c + 1) * N], x1[:, c * P:(c + 1) * P], mix[:, :],
                                   start=True, stop=True)
                mm.then_inc(mix_done, 1)

            def l2(s, k):
                if k >= 1:
                    pe.wait_ge(x3_made, s)
                for n, (x, w) in enumerate(((x2T_hi, w2_hi), (x2T_hi, w2_lo), (x2T_lo, w2_hi))):
                    if n == 0:
                        pe.wait_ge(w2_hi_made, 2 * s + 2)
                    if n == 1:
                        pe.wait_ge(w2_lo_made, 2 * s + 2)
                    if n == 2:
                        pe.wait_ge(x2T_lo_made, s + 1)
                    for c in range(C):
                        if n == 0 and c in (0, C // 2):
                            pe.wait_ge(x2T_hi_made, 2 * s + 1 + c // (C // 2))
                        mm = pe.matmul(ps_l2[:, :], x[:, c * N:(c + 1) * N], w[:, c * D:(c + 1) * D],
                                       start=(n == 0 and c == 0), stop=(n == 2 and c == C - 1))
                mm.then_inc(l2_done, 1)

            def transpose_x3(s, k, j):
                pe.wait_ge(x3_made, s + 1)
                if k >= 1:
                    pe.wait_ge(x3T_made, s)
                for c in range(C):
                    mm = pe.transpose(ps_x3T[:, c * N:(c + 1) * N], x3[j % YB][:, c * P:(c + 1) * P], ident[:, :])
                mm.then_inc(x3T_done, 1)

            def down(s, k, lang):
                pe.wait_ge(x3T_made, s + 1)
                if k >= 1:
                    pe.wait_ge(h_made, s)
                for c in range(C):
                    mm = pe.matmul(ps_h[:, :], x3T[:, c * N:(c + 1) * N],
                                   w1_sb[:, bass.ds(lang * (C * A) + c * A, A)], start=(c == 0), stop=(c == C - 1))
                mm.then_inc(h_done, 1)

            def transpose_h(s, k):
                pe.wait_ge(h_made, s + 1)
                if k >= 1:
                    pe.wait_ge(hT_made, s)
                pe.transpose(ps_hT[:, :], h[:, :], ident[:, :]).then_inc(hT_done, 1)

            def up(s, k, lang):
                pe.wait_ge(hT_made, s + 1)
                if k >= 1:
                    pe.wait_ge(y_made, s)
                pe.matmul(ps_up[:, :], hT[:, :], wup_sb[:, bass.ds(lang * D, D)], start=True, stop=True)\
                    .then_inc(up_done, 1)

            pe.wait_ge(dt_made, 1)
            pe.wait_ge(consts_made, 3)
            l0(0, 0, 0, 1)
            l0(0, 0, 1, 1)
            rotate(0, 0)
            l2(0, 0)

            def step(s, k, j):
                if k < LAST:
                    ordinal = ordinal_of(pe, s + 1)
                    l0(s + 1, k + 1, 0, ordinal)
                transpose_x3(s, k, j)
                if k < LAST:
                    l0(s + 1, k + 1, 1, ordinal)
                lang = language_of(pe, s)
                lang_before = language_of(pe, s - 1) if k >= 1 else None
                if k == 0:
                    pe.wait_ge(w1_loaded, 16)
                down(s, k, lang)
                if k < LAST:
                    rotate(s + 1, k + 1)
                transpose_h(s, k)
                if k == 1:
                    pe.wait_ge(wup_loaded, 16)
                if k >= 1:
                    up(s - 1, k - 1, lang_before)
                if k < LAST:
                    l2(s + 1, k + 1)

            over_samples(step)(pe)
            up(LAST, LAST, language_of(pe, LAST))


def kernel(**inputs):
    import numpy as _np
    import concourse.bacc as _bacc
    from concourse import mybir as _mybir
    from concourse.bass_utils import run_bass_kernel_spmd as _run

    a = {name: _np.asarray(v) for name, v in inputs.items()}
    x = a["x"]
    B, N, D = x.shape
    P = 128
    C = D // P

    def feature_major(w):
        n, _, cols = w.shape
        return w.reshape(n, C, P, cols).transpose(0, 2, 1, 3)

    arrays = {
        "xT": feature_major(x.transpose(0, 2, 1)),
        "subject": a["itok_B_0_7"].reshape(1, B),
        "category": a["itok_B_0_63"].reshape(1, B),
        "language": a["itok_B_0_8"].reshape(1, B),
        "delta_t": a["condB_deltat"].reshape(1, B),
        "W0T": feature_major(a["L0_cond_weight"].transpose(0, 2, 1)),
        "b0": a["L0_cond_bias"],
        "amp_tok": _np.repeat(a["L1_cond_amplitudes"], 2).reshape(N, 1),
        "freq_tok": _np.repeat(a["L1_cond_frequencies"], 2).reshape(N, 1),
        "W2": feature_major(a["L2_cond_W"]),
        "b2": a["L2_cond_b"],
        "W1": feature_major(a["L3_cond_W1"]).transpose(1, 0, 2, 3),
        "b1T": a["L3_cond_b1"].transpose(1, 0),
        "Wup": a["L3_cond_W2"].transpose(1, 0, 2),
        "bup": a["L3_cond_b2"],
        "gamma": a["L3_cond_gamma"],
        "beta": a["L3_cond_beta"],
    }
    nc = _bacc.Bacc("TRN2", target_bir_lowering=False, num_devices=1,
                     dynamic_dma_scratch_size=1024)
    args = []
    for name in arrays:
        arrays[name] = _np.ascontiguousarray(arrays[name])
        args.append(nc.dram_tensor(name, arrays[name].shape, _mybir.dt.from_np(arrays[name].dtype),
                                   kind="ExternalInput").ap())
    args.append(nc.dram_tensor("out", (B, N, D), fp32, kind="ExternalOutput").ap())
    conditioned_residual_stack(nc, *args)
    r = _run(nc, [arrays], core_ids=[0])
    return r.results[0]["out"]
```
